# Optimizing a Trainium2 kernel written in Bass

```python
import numpy as np
import jax
import jax.numpy as jnp

def _softmax(x, axis=-1):
    return jax.nn.softmax(x, axis=axis)

def _gelu(x):
    return jax.nn.gelu(x, approximate=True)

def _silu(x):
    return jax.nn.silu(x)

def _sigmoid(x):
    return jax.nn.sigmoid(x)

def _layernorm(x, axis=-1, eps=1e-05):
    m = jnp.mean(x, axis=axis, keepdims=True)
    v = jnp.var(x, axis=axis, keepdims=True)
    return (x - m) / jnp.sqrt(v + eps)

def _scatter_add(tgt, idx, src, axis=0):
    return tgt.at[idx].add(src)

def _segment_sum(src, seg, n):
    return jax.ops.segment_sum(src, seg, n)
kernel_name = 'mk_cond_seq_d1_seqx_r4_7ba63e'

def setup_inputs(seed: int=0):
    np.random.seed(seed)
    _w = jnp.asarray

    def _rec_inputs():
        import jax
        import jax.numpy as jnp
        _rk = jax.random.key(seed)
        x = -0.0003482 + 1 * jax.random.normal(jax.random.fold_in(_rk, 1), (32, 256, 288), jnp.float32)
        _lenS = 256 - jax.random.randint(jax.random.fold_in(_rk, 7), (32,), 0, max(1, 256 // 4) + 1, jnp.int32)
        _lenS2 = 256 - jax.random.randint(jax.random.fold_in(_rk, 8), (32,), 0, max(1, 256 // 4) + 1, jnp.int32)
        cond_1152 = 0.00257642 + 1.0011 * jax.random.normal(jax.random.fold_in(_rk, 11), (32, 288), jnp.float32)
        return (x, cond_1152)
    x, cond_1152 = _rec_inputs()

    def _L0_cond_setup():
        import jax, jax.numpy as jnp
        import numpy as np
        from jax.scipy.linalg import expm
        N, D, COND_DIM = (288, 64, 288)
        B, T = (16, 256)

        def _rotation(cond, W, b):
            v = jax.nn.silu(cond) @ W.T + b
            iu, ju = jnp.triu_indices(D, k=1)
            A = jnp.zeros((cond.shape[0], D, D), dtype=v.dtype)
            A = A.at[:, iu, ju].set(v).at[:, ju, iu].set(-v)
            return expm(A)
        key = jax.random.key(seed)
        k1, k2, k3, k4, k5 = jax.random.split(key, 5)
        x = jax.random.normal(k1, (B, T, N), dtype=jnp.float32)
        cond = jax.random.normal(k2, (B, COND_DIM), dtype=jnp.float32)
        P = jax.random.normal(k3, (N, D), dtype=jnp.float32)
        n_skew = D * (D - 1) // 2
        bound = 1.0 / np.sqrt(COND_DIM)
        W = jax.random.uniform(k4, (n_skew, COND_DIM), minval=-bound, maxval=bound, dtype=jnp.float32)
        b = jax.random.uniform(k5, (n_skew,), minval=-bound, maxval=bound, dtype=jnp.float32)
        return {'x': x, 'cond': cond, 'P': P, 'W': W, 'b': b}
    _L0_cond_all = _L0_cond_setup()
    _L0_cond_in = {k: v for k, v in _L0_cond_all.items() if k in ('P', 'W', 'b')}
    del _L0_cond_all
    return {'x': x, 'cond_1152': cond_1152, 'L0_cond_P': _L0_cond_in['P'], 'L0_cond_W': _L0_cond_in['W'], 'L0_cond_b': _L0_cond_in['b']}

def reference(x, cond_1152, L0_cond_P, L0_cond_W, L0_cond_b):
    import jax
    import jax.numpy as jnp

    def _L0_cond_ref(x, cond, P, W, b):
        import jax, jax.numpy as jnp
        import numpy as np
        from jax.scipy.linalg import expm
        N, D, COND_DIM = (288, 64, 288)
        B, T = (16, 256)

        def _rotation(cond, W, b):
            v = jax.nn.silu(cond) @ W.T + b
            iu, ju = jnp.triu_indices(D, k=1)
            A = jnp.zeros((cond.shape[0], D, D), dtype=v.dtype)
            A = A.at[:, iu, ju].set(v).at[:, ju, iu].set(-v)
            return expm(A)
        U, _ = jnp.linalg.qr(P)
        R = _rotation(cond, W, b)
        z = jnp.einsum('btn,nd->btd', x, U)
        z_rot = jnp.einsum('btd,bde->bte', z, R)
        x_rot = x + jnp.einsum('btd,nd->btn', z_rot - z, U)
        return x_rot
    x = _L0_cond_ref(x, cond_1152, L0_cond_P, L0_cond_W, L0_cond_b)
    return x

_drawn_inputs = setup_inputs


def setup_inputs(seed=0):
    import zlib

    import numpy as np

    out = dict(_drawn_inputs(seed))
    spreads = {}
    factors = {}
    for name, (base, spread) in spreads.items():
        noise = np.random.default_rng([zlib.crc32(name.encode()), seed]).standard_normal(out[name].shape)
        drawn = base * np.exp(spread * noise) if base else spread * noise
        out[name] = jnp.asarray(drawn.astype(out[name].dtype))
    for name, factor in factors.items():
        out[name] = (out[name] * factor).astype(out[name].dtype)
    return out
```

```python
from contextlib import ExitStack

import concourse.bass as bass
from concourse import mybir

F32 = mybir.dt.float32
F32R = mybir.dt.float32r
I32 = mybir.dt.int32
ALU = mybir.AluOpType
ACT = mybir.ActivationFunctionType
AX = mybir.AxisListType

NB = 32
T = 256
N = 288
D = 64
NC = 3
KC = N // NC
GB = 2
NG = NB // GB
BT = GB * T
NQ = NB // 2
PG = 4
NPG = NQ // PG
HALF_I = D // 2

LEVELS = 4
EXTRA = 10
NORM_LIMIT = 19.0
NEWTON = 6
SWEEPS = 12
GENERAL_NEWTON = 24
NEWTON_TOL = 1e-4
SIGN_MARGIN = 256.0

C0, C1, C2, C3, C4 = 1 / 2, 1 / 24, 1 / 720, 1 / 40320, 1 / 3628800
S0, S1, S2, S3, S4 = 1.0, 1 / 6, 1 / 120, 1 / 5040, 1 / 362880


def rotation_kernel(nc, xb, cond, pc, pt, wd, bd, out):
    with ExitStack() as ctx:
        def sb(name, shape, dt=F32):
            return ctx.enter_context(nc.sbuf_tensor(name, shape, dt))

        def sem(name):
            return ctx.enter_context(nc.semaphore(name))

        x = sb("x", [KC, NG, NC, BT])
        room = sb("room", [128, NC * HALF_I * 2 * D])
        wsym = room[0:KC + 1, :].rearrange("p (c i j) -> p c i j", c=NC, i=HALF_I)
        bdz2 = room[:, 0:2048].rearrange("p (q d) -> p q d", q=NQ)
        tmp = room[0:KC, 0:2 * BT].rearrange("p (r t) -> p r t", r=2)
        bdz = room[:, 2048:4096].rearrange("p (q d) -> p q d", q=NQ)
        fs = room[0:D, 4096:8192].rearrange("p (b k d) -> p b k d", b=NB, k=2)
        z = room[:, 4096:5120].rearrange("p (q d) -> p q d", q=NQ)
        z2 = room[:, 5120:6144].rearrange("p (q d) -> p q d", q=NQ)
        vv = room[:, 6144:8192].rearrange("p (q k d) -> p q k d", q=NQ, k=2)
        em = room[:, 8192:9216].rearrange("p (q d) -> p q d", q=NQ)
        sc = room[:, 9216:11264].rearrange("p (q k d) -> p q k d", q=NQ, k=2)
        sq = room[:, 11264:12288].rearrange("p (q d) -> p q d", q=NQ)
        y = sb("y", [D, NB, T])
        pcs = sb("pcs", [KC, NC, D])
        pts = sb("pts", [D, N])
        cnd = sb("cnd", [KC, NC, NB])
        cexp = sb("cexp", [KC, NC, NB])
        silu = sb("silu", [KC + 1, NC, NB])
        ident = sb("ident", [128, 128])
        neg3 = sb("neg3", [D, D])
        pos2 = sb("pos2", [D, D])
        phi = sb("phi", [D, D])
        su = sb("su", [D, D])
        suh = sb("suh", [D, D])
        colm = sb("colm", [D, 2 * D])
        onesm = sb("onesm", [128, 128])
        halfm = sb("halfm", [128, 128])
        sgnm = sb("sgnm", [128, D])
        gs = sb("gs", [D, 2 * D])
        xx = sb("xx", [D, 2 * D])
        tm = sb("tm", [D, D])
        mm = sb("mm", [D, 2 * D])
        junk = sb("junk", [D, 2 * D])
        small = sb("small", [D, 8])
        qq = sb("qq", [D, 2 * D])
        qh = sb("qh", [D, 1])
        cc = sb("cc", [D, 2 * D])
        cl = sb("cl", [D, 2 * D])
        ul = sb("ul", [D, 2 * D])
        ul2 = sb("ul2", [D, 2 * D])
        hp = sb("hp", [D, 1])
        uh = sb("uh", [D, 1])
        ur = sb("ur", [D, 1])
        stats = sb("stats", [D, 4])
        st1 = sb("st1", [1, 8])
        redo_qr = sb("redo_qr", [1, 1], I32)
        phij = sb("phij", [D, D])
        inact = sb("inact", [D, D])
        sg = sb("sg", [128, 1])
        xd = sb("xd", [D, 2, D])
        bdx = sb("bdx", [128, 128])
        uuh = sb("uuh", [128, N], F32R)
        uul = sb("uul", [128, N], F32R)
        bm = sb("bm", [128, NQ, D])
        fro = sb("fro", [128, NQ])
        over = sb("over", [128, NQ])
        cnt = sb("cnt", [128, 1])
        fac = sb("fac", [128, 1])
        more = sb("more", [1, 1], I32)
        bdb = sb("bdb", [128, NQ, 128])
        wst = sb("wst", [128, 2, BT], F32R)

        ps = [ctx.enter_context(nc.psum_tensor(f"ps{i}", [128, 512], F32)) for i in range(8)]
        pq = ps[0:2]
        py = ps[2:4]
        pe_ = ps[4:8]

        p_in, pt_in, c_in = sem("p_in"), sem("pt_in"), sem("c_in")
        w_in = [sem(f"w_in{i}") for i in range(4)]
        b_in = sem("b_in")
        x_in = [sem("x_in0"), sem("x_in1")]
        masks = sem("masks")
        pool_chain = sem("pool_chain")
        ones_row = sem("ones_row")
        exp_done, silu_done = sem("exp_done"), sem("silu_done")
        dv = sem("dv")
        g_ps, gdiag, groot = sem("g_ps"), sem("gdiag"), sem("groot")
        qr_mm, qr_sb = sem("qr_mm"), sem("qr_sb")
        y_mm, y_sb = sem("y_mm"), sem("y_sb")
        v_mm, b_sb = sem("v_mm"), sem("b_sb")
        sq_done, fro_sb, fro_mm, over_sb, cnt_mm = sem("sq_done"), sem("fro_sb"), sem("fro_mm"), sem("over_sb"), sem("cnt_mm")
        bd0, bdz_clear = sem("bd0"), sem("bdz_clear")
        flags = sem("flags")
        st_mm, st_sb = sem("st_mm"), sem("st_sb")
        ex_mm = sem("ex_mm")
        ex_act, ex_dve, ex_pool = sem("ex_act"), sem("ex_dve"), sem("ex_pool")
        gen_mm, gen_sb, gen_dv = sem("gen_mm"), sem("gen_sb"), sem("gen_dv")
        xtra_mm, xtra_sb = sem("xtra_mm"), sem("xtra_sb")
        final = sem("final")
        uu_mm, uu_sb = sem("uu_mm"), sem("uu_sb")
        em_sb, f_mm, f_sb = sem("em_sb"), sem("f_mm"), sem("f_sb")
        w_mm, w_hi, w_lo = sem("w_mm"), sem("w_hi"), sem("w_lo")
        o_mm, o_dve, o_act, o_pool = sem("o_mm"), sem("o_dve"), sem("o_act"), sem("o_pool")
        stored = sem("stored")

        block = ctx.enter_context(nc.Block())

        NMASK = 20

        @block.sync
        def _(sp):
            sp.dma_start(pcs[:, :, :], pc).then_inc(p_in, 16)
            sp.dma_start(pts[:, :], pt).then_inc(pt_in, 16)
            sp.dma_start(cnd[:, :, :], cond).then_inc(c_in, 16)
            sp.dma_start(x[:, 0, :, :], xb[0, :, :, :]).then_inc(x_in[0], 16)
            sp.dma_start(x[:, 1, :, :], xb[1, :, :, :]).then_inc(x_in[1], 16)
            sp.dma_start(wsym[KC:KC + 1, 0, :, :], bd).then_inc(b_in, 16)

            WQ = HALF_I // 4
            for k in range(4):
                for r in range(2):
                    g = 2 + 2 * k + r
                    sp.wait_ge(x_in[r], 16 * (k + 1))
                    sp.dma_start(x[:, g, :, :], xb[g, :, :, :]).then_inc(x_in[r], 16)
                sp.dma_start(wsym[0:KC, :, k * WQ:(k + 1) * WQ, :], wd[:, :, k * WQ:(k + 1) * WQ, :]).then_inc(w_in[k], 16)
            for k in range(4, NG // 2 - 1):
                for r in range(2):
                    g = 2 + 2 * k + r
                    sp.wait_ge(x_in[r], 16 * (k + 1))
                    sp.dma_start(x[:, g, :, :], xb[g, :, :, :]).then_inc(x_in[r], 16)

            for g in range(NG):
                sp.wait_ge(o_dve, 2 * g + 2)
                sp.wait_ge(o_pool, g + 1)
                sp.dma_start(out[g, :, :, :], x[:, g, :, :]).then_inc(stored, 16)
            sp.wait_ge(stored, 16 * NG)

        @block.gpsimd
        def _(pool):
            n = [0]

            def link(ins):
                n[0] += 1
                ins.then_inc(pool_chain, 1)
                pool.wait_ge(pool_chain, n[0])

            link(nc.gpsimd.memset(mm[:, D:2 * D], 0.0))
            link(nc.gpsimd.memset(ident[:, :], 0.0))
            nc.gpsimd.affine_select(out=ident[:, :], in_=ident[:, :], compare_op=ALU.not_equal, fill=1.0,
                                    base=0, pattern=[[-1, 128]], channel_multiplier=1).then_inc(masks, 1)
            for dst, val in ((neg3, -3.0), (pos2, 2.0)):
                link(nc.gpsimd.memset(dst[:, :], 0.0))
                nc.gpsimd.affine_select(out=dst[:, :], in_=dst[:, :], compare_op=ALU.not_equal, fill=val,
                                        base=0, pattern=[[-1, D]], channel_multiplier=1).then_inc(masks, 1)
            for dst, val in ((phi, -1.0), (su, 1.0), (suh, 0.5)):
                link(nc.gpsimd.memset(dst[:, :], val))
                last = nc.gpsimd.affine_select(out=dst[:, :], in_=dst[:, :], compare_op=ALU.is_gt, fill=0.0,
                                               base=0, pattern=[[1, D]], channel_multiplier=-1)
                if dst is phi:
                    link(last)
                    last = nc.gpsimd.affine_select(out=dst[:, :], in_=dst[:, :], compare_op=ALU.not_equal, fill=-0.5,
                                                   base=0, pattern=[[-1, D]], channel_multiplier=1)
                last.then_inc(masks, 1)
            link(nc.gpsimd.memset(sgnm[:, :], 2.0 ** -LEVELS))
            for h in range(2):
                rows = sgnm[h * D:(h + 1) * D, :]
                link(nc.gpsimd.affine_select(out=rows, in_=rows, compare_op=ALU.is_ge, fill=-2.0 ** -LEVELS,
                                             base=0, pattern=[[1, D]], channel_multiplier=-1))
                link(nc.gpsimd.affine_select(out=rows, in_=rows, compare_op=ALU.not_equal, fill=0.0,
                                             base=0, pattern=[[-1, D]], channel_multiplier=1))
            link(nc.gpsimd.memset(colm[:, 0:D], 1.0))
            link(nc.gpsimd.memset(colm[:, D:2 * D], 0.0))
            link(nc.gpsimd.memset(onesm[:, :], 1.0))
            link(nc.gpsimd.memset(halfm[:, :], 0.0))
            for h in range(2):
                link(nc.gpsimd.memset(halfm[h * D:(h + 1) * D, h * D:(h + 1) * D], 1.0))
            link(nc.gpsimd.memset(bdx[:, :], 0.0))
            link(nc.gpsimd.memset(bdb[:, :, :], 0.0))
            nc.gpsimd.memset(silu[KC:KC + 1, :, :], 1.0).then_inc(masks, 1)
            pool.wait_ge(v_mm, 2)
            nc.gpsimd.memset(room[:, 0:4096], 0.0).then_inc(bdz_clear, 1)

            pool.wait_ge(b_sb, 8)
            nc.gpsimd.tensor_tensor(sq[:, :, :], bm[:, :, :], bm[:, :, :], ALU.mult).then_inc(sq_done, 1)

            with pool.Fori(0, LEVELS) as lv:
                for g in range(NPG):
                    qs = slice(g * PG, (g + 1) * PG)
                    pool.wait_ge(ex_dve, lv * NPG + (4 * NPG + g + 1))
                    nc.gpsimd.tensor_tensor(bdb[0:D, qs, 0:D], sc[0:D, qs, 0, :],
                                            onesm[0:D, 0:D].rearrange("p (a d) -> p a d", a=1).to_broadcast([D, PG, D]),
                                            ALU.mult).then_inc(ex_pool, 1)

            with pool.Fori(0, NG // 2) as h:
                for r in range(2):
                    pool.wait_ge(o_act, h * 2 + (r + 1))
                    xc = x[:, bass.ds(h * 2 + r, 1), 2, :]
                    nc.gpsimd.tensor_tensor(xc, xc, tmp[:, r:r + 1, :], ALU.add).then_inc(o_pool, 1)

        def f_copy(copy, k, h, *args):
            src = pe_[k][h * D:(h + 1) * D, :].rearrange("p (q a d) -> p q a d", q=8, a=1).to_broadcast([D, 8, 2, D])
            return copy(fs[:, h * NQ + k * 8:h * NQ + k * 8 + 8, :, :], src, *args)

        @block.scalar
        def _(act):
            act.wait_ge(c_in, 16)
            nc.scalar.activation(cexp[:, :, :], cnd[:, :, :], ACT.Exp, scale=-1.0).then_inc(exp_done, 1)
            act.wait_ge(gdiag, 1)
            nc.scalar.activation(small[:, 1:2], small[:, 0:1], ACT.Sqrt).then_inc(groot, 1)

            with act.Fori(0, NG // 2) as h:
                for r in range(2):
                    act.wait_ge(y_mm, h * 2 + (r + 1))
                    nc.scalar.activation(y[:, bass.ds(h * 4 + 2 * r, 2), :].rearrange("p a t -> p (a t)"),
                                         py[r][0:D, :], ACT.Copy).then_inc(y_sb, 1)

            for k, (dst, scale) in enumerate(((z, -1.0), (z2, 1.0))):
                for g in range(NPG):
                    qs = slice(g * PG, (g + 1) * PG)
                    act.wait_ge(ex_mm, k * NPG + g + 1)
                    nc.scalar.activation(dst[:, qs, :], pe_[g][:, 0:PG * D].rearrange("p (q d) -> p q d", q=PG),
                                         ACT.Copy, scale=scale).then_inc(ex_act, 1)
            for g in range(NPG):
                qs = slice(g * PG, (g + 1) * PG)
                act.wait_ge(ex_dve, 3 * NPG + g + 1)
                nc.scalar.activation(sc[:, qs, 1, :], pe_[g][:, PG * D:2 * PG * D].rearrange("p (q d) -> p q d", q=PG),
                                     ACT.Copy, scale=-2.0).then_inc(ex_act, 1)
            with act.Fori(0, LEVELS) as lv:
                for g in range(NPG):
                    qs = slice(g * PG, (g + 1) * PG)
                    pg = pe_[g][:, :].rearrange("p (q k d) -> p q k d", q=PG, k=2)
                    act.wait_ge(ex_dve, lv * NPG + (4 * NPG + g + 1))
                    nc.scalar.activation(bdb[D:128, qs, D:128], sc[D:128, qs, 0, :], ACT.Copy)
                    nc.scalar.activation(sc[:, qs, 1, :], pg[:, :, 0, :], ACT.Copy, scale=4.0).then_inc(ex_act, 1)

            act.wait_ge(f_mm, 2)
            for h in range(2):
                f_copy(nc.scalar.activation, 1, h, ACT.Copy).then_inc(f_sb, 1)

            for g in range(NG + 1):
                if g < NG:
                    act.wait_ge(w_mm, g + 1)
                    if g >= 2:
                        act.wait_ge(o_mm, 3 * (g - 1))
                    nc.scalar.activation(wst[:, g % 2, :], py[g % 2][:, :], ACT.Copy).then_inc(w_hi, 1)
                if g >= 1:
                    k = g - 1
                    act.wait_ge(o_mm, 3 * k + 3)
                    if k >= 2:
                        act.wait_ge(o_pool, k - 1)
                    nc.scalar.activation(tmp[:, k % 2, :], pe_[2 + k % 2][0:KC, :], ACT.Copy).then_inc(o_act, 1)

        def newton_dve(v, mmsem, sbsem, k, active=None, check=False):
            v.wait_ge(mmsem, k + 1)
            nc.vector.tensor_copy(tm[:, :], pq[0][0:D, 0:D]).then_inc(sbsem, 1)
            v.wait_ge(mmsem, k + 2)
            if active is None:
                nc.vector.tensor_tensor(mm[:, 0:D], pq[1][0:D, 0:D], phi[:, :], ALU.mult).then_inc(sbsem, 1)
            else:
                v.wait_ge(gen_dv, active - 1)
                nc.vector.tensor_tensor(junk[:, 0:D], pq[1][0:D, 0:D], phij[:, :], ALU.mult).then_inc(gen_dv, 1)
                v.wait_ge(gen_dv, active)
                nc.vector.tensor_tensor(mm[:, 0:D], junk[:, 0:D], inact[:, :], ALU.add).then_inc(sbsem, 1)
            if check:
                nc.vector.tensor_tensor(junk[:, 0:D], pq[1][0:D, 0:D], pos2[:, :], ALU.add).then_inc(gdiag, 1)
            v.wait_ge(mmsem, k + 3)
            nc.vector.tensor_copy(xx[:, :], pq[0][0:D, 0:2 * D]).then_inc(sbsem, 1)

        def newton_pe(pe, mmsem, sbsem, k, filler=None):
            f = filler or (lambda: None)
            pe.wait_ge(sbsem, k)
            nc.tensor.matmul(pq[0][:, 0:D], gs[:, :], xx[:, 0:D], start=True, stop=True).then_inc(mmsem, 1)
            nc.tensor.matmul(pq[1][:, 0:D], ident[0:D, :], neg3[:, :], start=True, stop=False)
            f()
            pe.wait_ge(sbsem, k + 1)
            nc.tensor.matmul(pq[1][:, 0:D], xx[:, :], tm[:, :], start=False, stop=True).then_inc(mmsem, 1)
            f()
            pe.wait_ge(sbsem, k + 2)
            nc.tensor.matmul(pq[0][:, D:2 * D], mm[:, :], xx[:, D:2 * D], start=True, stop=True)
            nc.tensor.matmul(pq[0][0:D, 0:D], xx[:, D:2 * D], mm[:, 0:D], start=True, stop=True).then_inc(mmsem, 1)
            f()

        def q1_pe(mmsem):
            nc.tensor.matmul(pq[1][0:D, 0:D], pts[:, 0:D], xx[:, 0:D], start=True, stop=True)
            nc.tensor.matmul(pq[1][0:D, D:2 * D], xx[:, 0:D], pts[:, 0:D], start=True, stop=True).then_inc(mmsem, 1)

        def q1_dve(v, mmsem, k, sbsem, dvsem, base):
            v.wait_ge(mmsem, k)
            nc.vector.tensor_copy(qq[:, :], pq[1][0:D, 0:2 * D]).then_inc(dvsem, 1)
            v.wait_ge(dvsem, base + 1)
            nc.vector.tensor_tensor_reduce(out=junk[:, 0:D], in0=qq[:, 0:D], in1=ident[0:D, 0:D], scale=0.5, scalar=-0.5,
                                           op0=ALU.mult, op1=ALU.add, accum_out=qh[:, 0:1]).then_inc(dvsem, 1)
            v.wait_ge(dvsem, base + 2)
            nc.vector.memset(ul[:, :], 0.0).then_inc(sbsem, 1)

        def sweep_pe(pe, mmsem, sbsem, k):
            pe.wait_ge(sbsem, k)
            nc.tensor.matmul(pq[0][:, D:2 * D], ul[:, :], ul[:, D:2 * D], start=True, stop=True)
            nc.tensor.matmul(pq[0][0:D, 0:D], ul[:, D:2 * D], ul[:, 0:D], start=True, stop=True).then_inc(mmsem, 1)

        SWEEP_DV = 5

        def sweep_dve(v, mmsem, k, sbsem, dvsem, base, dst):
            v.wait_ge(mmsem, k)
            nc.vector.tensor_tensor_reduce(out=junk[:, 0:D], in0=pq[0][0:D, 0:D], in1=ident[0:D, 0:D],
                                           scale=-0.5, scalar=qh[:, 0:1], op0=ALU.mult, op1=ALU.add,
                                           accum_out=hp[:, 0:1]).then_inc(dvsem, 1)
            nc.vector.tensor_tensor(cc[:, :], qq[:, :], pq[0][0:D, 0:2 * D], ALU.subtract).then_inc(dvsem, 1)
            v.wait_ge(dvsem, base + 1)
            nc.vector.scalar_tensor_tensor(out=uh[:, :], in0=hp[:, :], scalar=-0.5, in1=hp[:, :],
                                           op0=ALU.is_ge, op1=ALU.add).then_inc(dvsem, 1)
            v.wait_ge(dvsem, base + 2)
            nc.vector.tensor_scalar(cl[:, :], cc[:, :], 4.0, -4.0, ALU.min, ALU.max).then_inc(dvsem, 1)
            v.wait_ge(dvsem, base + 3)
            nc.vector.reciprocal(ur[:, :], uh[:, :]).then_inc(dvsem, 1)
            v.wait_ge(dvsem, base + 4)
            nc.vector.tensor_tensor(dst[:, 0:D], cl[:, 0:D], su[:, :], ALU.mult)
            v.wait_ge(dvsem, base + 5)
            nc.vector.scalar_tensor_tensor(out=dst[:, D:2 * D], in0=cl[:, D:2 * D], scalar=ur[:, 0:1],
                                           in1=suh[:, :], op0=ALU.mult, op1=ALU.mult).then_inc(sbsem, 1)

        GEN_STEPS = D * GENERAL_NEWTON
        GEN_X = 3 * GEN_STEPS + 1

        def general_dve(v):
            for h in range(2):
                last = nc.vector.tensor_scalar(xx[:, h * D:(h + 1) * D], ident[0:D, 0:D], small[:, 2:3], None, ALU.mult)
            last.then_inc(gen_sb, 1)
            with v.Fori(0, D) as j:
                per = GENERAL_NEWTON + 3
                upto = colm[:, bass.ds(D - 1 - j, D)]
                nc.vector.tensor_tensor(phij[:, :], phi[:, :], upto, ALU.mult).then_inc(gen_dv, 1)
                nc.vector.tensor_tensor(junk[:, 0:D], ident[0:D, 0:D], upto, ALU.mult).then_inc(gen_dv, 1)
                v.wait_ge(gen_dv, j * per + 2)
                nc.vector.tensor_tensor(inact[:, :], ident[0:D, 0:D], junk[:, 0:D], ALU.subtract).then_inc(gen_dv, 1)
                with v.Fori(0, GENERAL_NEWTON) as i:
                    newton_dve(v, gen_mm, gen_sb, j * (3 * GENERAL_NEWTON) + i * 3, active=j * per + (i + 4))
            base = D * (GENERAL_NEWTON + 3)
            q1_dve(v, gen_mm, GEN_X, gen_sb, gen_dv, base)
            with v.Fori(0, D) as i:
                sweep_dve(v, gen_mm, i + (GEN_X + 1), gen_sb, gen_dv, i * SWEEP_DV + (base + 2), ul)

        def general_pe(pe):
            with pe.Fori(0, GEN_STEPS) as n:
                newton_pe(pe, gen_mm, gen_sb, n * 3 + 1)
            pe.wait_ge(gen_sb, GEN_X)
            q1_pe(gen_mm)
            with pe.Fori(0, D) as i:
                sweep_pe(pe, gen_mm, gen_sb, i + (GEN_X + 1))

        @block.vector
        def _(v):
            count = [0]

            def out_(ins):
                ins.then_inc(dv, 1)
                count[0] += 1
                return count[0]

            def start_x():
                for h in range(2):
                    last = nc.vector.tensor_scalar(xx[:, h * D:(h + 1) * D], ident[0:D, 0:D], small[:, 2:3], None, ALU.mult)
                return last

            v.wait_ge(masks, 1)
            v.wait_ge(g_ps, 1)
            nc.vector.tensor_tensor_reduce(out=junk[:, 0:D], in0=pq[0][0:D, 0:D], in1=ident[0:D, 0:D],
                                           scale=1.0, scalar=0.0, op0=ALU.mult, op1=ALU.add,
                                           accum_out=small[:, 0:1]).then_inc(gdiag, 1)
            for h in range(2):
                nc.vector.tensor_copy(gs[:, h * D:(h + 1) * D], pq[0][0:D, 0:D])
            v.wait_ge(groot, 1)
            v.wait_ge(dv, out_(nc.vector.reciprocal(small[:, 2:3], small[:, 1:2])))
            start_x().then_inc(qr_sb, 1)

            v.wait_ge(exp_done, 1)
            v.wait_ge(dv, out_(nc.vector.tensor_scalar(cexp[:, :, :], cexp[:, :, :], 1.0, None, ALU.add)))
            v.wait_ge(dv, out_(nc.vector.reciprocal(cexp[:, :, :], cexp[:, :, :])))
            nc.vector.tensor_tensor(silu[0:KC, :, :], cnd[:, :, :], cexp[:, :, :], ALU.mult).then_inc(silu_done, 1)

            v.wait_ge(masks, 7)
            with v.Fori(0, NEWTON - 1) as i:
                newton_dve(v, qr_mm, qr_sb, i * 3)
            newton_dve(v, qr_mm, qr_sb, 3 * (NEWTON - 1), check=True)
            v.wait_ge(gdiag, 2)
            nc.vector.tensor_reduce(stats[:, 0:1], junk[:, 0:D], AX.X, ALU.max, apply_absolute_value=True)
            k = 3 * NEWTON + 1
            q1_dve(v, qr_mm, k, qr_sb, dv, count[0])
            count[0] += 2

            base = count[0]
            with v.Fori(0, SWEEPS) as i:
                sweep_dve(v, qr_mm, i + (k + 1), qr_sb, dv, i * SWEEP_DV + base, ul)
            count[0] += SWEEPS * SWEEP_DV
            k += SWEEPS + 1
            sweep_dve(v, qr_mm, k, qr_sb, dv, count[0], ul2)
            count[0] += SWEEP_DV
            v.wait_ge(qr_sb, k + 1)
            v.wait_ge(dv, out_(nc.vector.tensor_tensor(junk[:, :], ul[:, :], ul2[:, :], ALU.subtract)))
            v.wait_ge(dv, out_(nc.vector.tensor_scalar(small[:, 4:5], hp[:, :], 2.0, 1.0, ALU.mult, ALU.add)))
            v.wait_ge(dv, out_(nc.vector.tensor_reduce(small[:, 5:6], junk[:, :], AX.X, ALU.max, apply_absolute_value=True)))
            v.wait_ge(dv, out_(nc.vector.tensor_scalar(stats[:, 1:2], small[:, 5:6], SIGN_MARGIN, None, ALU.mult)))
            nc.vector.tensor_reduce(stats[:, 2:3], small[:, 4:5], AX.X, ALU.max, apply_absolute_value=True, negate=True).then_inc(st_sb, 1)
            v.wait_ge(st_mm, 1)
            v.wait_ge(dv, out_(nc.vector.tensor_reduce(st1[0:1, 0:3], pq[1][0:1, 0:3 * D].rearrange("p (k d) -> p k d", k=3), AX.X, ALU.max)))
            v.wait_ge(dv, out_(nc.vector.tensor_tensor(st1[0:1, 3:4], st1[0:1, 1:2], st1[0:1, 2:3], ALU.add)))
            v.wait_ge(dv, out_(nc.vector.tensor_scalar(st1[0:1, 4:5], st1[0:1, 3:4], 0.0, None, ALU.is_le)))
            v.wait_ge(dv, out_(nc.vector.scalar_tensor_tensor(out=st1[0:1, 5:6], in0=st1[0:1, 0:1], scalar=NEWTON_TOL,
                                                              in1=st1[0:1, 4:5], op0=ALU.is_le, op1=ALU.mult)))
            nc.vector.tensor_scalar(redo_qr[0:1, 0:1], st1[0:1, 5:6], -1.0, 1.0, ALU.mult, ALU.add).then_inc(flags, 1)
            v.wait_ge(flags, 1)
            redo = v.value_load(redo_qr[0:1, 0:1], min_val=0, max_val=1)
            with v.If(redo):
                general_dve(v)
            for h in range(2):
                last = nc.vector.tensor_copy(xd[:, h, :], xx[:, 0:D])
            last.then_inc(final, 1)
            nc.vector.tensor_scalar(sg[0:D, :], uh[:, :], 0.0, -2.0, ALU.is_ge, ALU.mult).then_inc(final, 1)
            nc.vector.tensor_scalar(sg[D:128, :], uh[:, :], 0.0, -2.0, ALU.is_ge, ALU.mult).then_inc(final, 1)
            v.wait_ge(final, 3)
            nc.vector.tensor_scalar(sg[:, :], sg[:, :], 1.0, None, ALU.add).then_inc(final, 1)
            v.wait_ge(final, 4)
            for h in range(2):
                nc.vector.tensor_scalar(bdx[h * D:(h + 1) * D, h * D:(h + 1) * D], xx[:, D:2 * D], sg[0:D, 0:1], None,
                                        ALU.mult).then_inc(final, 1)
            v.wait_ge(uu_mm, 1)
            nc.vector.tensor_scalar(uuh[:, :], pq[1][:, 0:N], sg[:, 0:1], None, ALU.mult).then_inc(uu_sb, 1)
            v.wait_ge(uu_sb, 1)
            nc.vector.scalar_tensor_tensor(out=uul[:, :], in0=pq[1][:, 0:N], scalar=sg[:, 0:1], in1=uuh[:, :].bitcast(F32),
                                           op0=ALU.mult, op1=ALU.subtract).then_inc(uu_sb, 1)

            for ib in range(2):
                v.wait_ge(v_mm, ib + 1)
                for i2 in range(2):
                    src = pe_[ib][i2 * D:(i2 + 1) * D, :].rearrange("p (i b) -> p b i", i=16)
                    c0 = i2 * HALF_I + ib * 16
                    for h in range(2):
                        nc.vector.tensor_tensor(
                            bm[h * D:(h + 1) * D, :, c0:c0 + 16], src[:, h * NQ:(h + 1) * NQ, :],
                            sgnm[i2 * D:(i2 + 1) * D, c0:c0 + 16].rearrange("p (a c) -> p a c", a=1).to_broadcast([D, NQ, 16]),
                            ALU.mult).then_inc(b_sb, 1)
            v.wait_ge(sq_done, 1)
            nc.vector.tensor_reduce(fro[:, :], sq[:, :, :], AX.X, ALU.add).then_inc(fro_sb, 1)
            v.wait_ge(fro_mm, 1)
            nc.vector.tensor_scalar(over[:, :], pe_[2][:, 0:NQ], 2 * NORM_LIMIT ** 2 / 4.0 ** LEVELS, None,
                                    ALU.is_gt).then_inc(over_sb, 1)
            v.wait_ge(cnt_mm, 1)
            v.wait_ge(dv, out_(nc.vector.tensor_reduce(cnt[:, :], pe_[3][:, 0:NQ], AX.X, ALU.max)))
            v.wait_ge(dv, out_(nc.vector.tensor_scalar(fac[:, :], cnt[:, :], 0.0, 2.0 ** -EXTRA - 1.0, ALU.is_gt, ALU.mult)))
            nc.vector.tensor_scalar(more[0:1, 0:1], cnt[0:1, :], 0.0, None, ALU.is_gt).then_inc(flags, 1)
            v.wait_ge(dv, out_(nc.vector.tensor_scalar(fac[:, :], fac[:, :], 1.0, None, ALU.add)))
            for h in range(2):
                last = out_(nc.vector.tensor_scalar(bdb[h * D:(h + 1) * D, :, h * D:(h + 1) * D], bm[h * D:(h + 1) * D, :, :],
                                                    fac[h * D:(h + 1) * D, 0:1], None, ALU.mult))
            v.wait_ge(dv, last)
            nc.vector.tensor_scalar(bm[:, :, :], bm[:, :, :], fac[:, 0:1], None, ALU.mult).then_inc(bd0, 1)

            def pview(g, n):
                return pe_[g][:, 0:PG * n].rearrange("p (q d) -> p q d", q=PG)

            def diag_from_psum(dst, g, off, scale):
                qs = slice(g * PG, (g + 1) * PG)
                for h in range(2):
                    last = nc.vector.tensor_scalar(
                        dst[h * D:(h + 1) * D, qs, h * D:(h + 1) * D],
                        pe_[g][h * D:(h + 1) * D, off:off + PG * D].rearrange("p (q d) -> p q d", q=PG), scale, None, ALU.mult)
                return last

            v.wait_ge(bdz_clear, 1)
            for g in range(NPG):
                v.wait_ge(ex_act, g + 1)
                diag_from_psum(bdz, g, 0, -1.0).then_inc(ex_dve, 1)
            for g in range(NPG):
                qs = slice(g * PG, (g + 1) * PG)
                v.wait_ge(ex_act, NPG + g + 1)
                diag_from_psum(bdz2, g, 0, 1.0)
                nc.vector.scalar_tensor_tensor(out=sc[:, qs, 0, :], in0=z2[:, qs, :], scalar=C4 / C3, in1=z[:, qs, :],
                                               op0=ALU.mult, op1=ALU.add)
                nc.vector.scalar_tensor_tensor(out=sc[:, qs, 1, :], in0=z2[:, qs, :], scalar=S4 / S3, in1=z[:, qs, :],
                                               op0=ALU.mult, op1=ALU.add).then_inc(ex_dve, 1)
            idb = [ident[h * D:(h + 1) * D, h * D:(h + 1) * D].rearrange("p (a c) -> p a c", a=1).to_broadcast([D, NQ, D]) for h in range(2)]
            for k, (c0, c1, c2) in enumerate(((C0, C1, C2), (S0, S1, S2))):
                v.wait_ge(dv, out_(nc.vector.tensor_scalar(vv[:, :, k, :], z[:, :, :], c1, None, ALU.mult)))
                v.wait_ge(dv, out_(nc.vector.scalar_tensor_tensor(out=vv[:, :, k, :], in0=z2[:, :, :], scalar=c2, in1=vv[:, :, k, :],
                                                                  op0=ALU.mult, op1=ALU.add)))
                for h in range(2):
                    hs = slice(h * D, (h + 1) * D)
                    last = out_(nc.vector.scalar_tensor_tensor(out=vv[hs, :, k, :], in0=idb[h], scalar=c0, in1=vv[hs, :, k, :],
                                                               op0=ALU.mult, op1=ALU.add))
                v.wait_ge(dv, last)
            for g in range(NPG):
                qs = slice(g * PG, (g + 1) * PG)
                pg = pe_[g][:, :].rearrange("p (q k d) -> p q k d", q=PG, k=2)
                v.wait_ge(ex_mm, 2 * NPG + g + 1)
                for k, c3 in ((0, C3), (1, S3)):
                    last = nc.vector.scalar_tensor_tensor(out=sc[:, qs, k, :], in0=pg[:, :, k, :], scalar=c3,
                                                          in1=vv[:, qs, k, :], op0=ALU.mult, op1=ALU.add)
                last.then_inc(ex_dve, 1)
            for g in range(NPG):
                qs = slice(g * PG, (g + 1) * PG)
                v.wait_ge(ex_mm, 3 * NPG + g + 1)
                diag_from_psum(bdb, g, 0, -1.0)
                nc.vector.tensor_scalar(sc[:, qs, 0, :], pview(g, D), -1.0, None, ALU.mult).then_inc(ex_dve, 1)
            with v.Fori(0, LEVELS) as lv:
                for g in range(NPG):
                    qs = slice(g * PG, (g + 1) * PG)
                    pg = pe_[g][:, :].rearrange("p (q k d) -> p q k d", q=PG, k=2)
                    v.wait_ge(ex_mm, lv * NPG + (4 * NPG + g + 1))
                    nc.vector.scalar_tensor_tensor(out=sc[:, qs, 0, :], in0=sc[:, qs, 0, :], scalar=2.0, in1=pg[:, :, 1, :],
                                                   op0=ALU.mult, op1=ALU.add).then_inc(ex_dve, 1)
            v.wait_ge(ex_act, (3 + LEVELS) * NPG)
            v.wait_ge(ex_pool, LEVELS * NPG)
            v.wait_ge(ex_dve, (4 + LEVELS) * NPG)
            deeper = v.value_load(more[0:1, 0:1], min_val=0, max_val=1)
            with v.If(deeper):
                with v.Fori(0, EXTRA) as lv:
                    for g in range(NPG):
                        qs = slice(g * PG, (g + 1) * PG)
                        pg = pe_[g][:, :].rearrange("p (q k d) -> p q k d", q=PG, k=2)
                        v.wait_ge(xtra_mm, lv * NPG + (g + 1))
                        nc.vector.scalar_tensor_tensor(out=sc[:, qs, 0, :], in0=sc[:, qs, 0, :], scalar=2.0, in1=pg[:, :, 1, :],
                                                       op0=ALU.mult, op1=ALU.add).then_inc(xtra_sb, 1)
                        nc.vector.tensor_scalar(sc[:, qs, 1, :], pg[:, :, 0, :], 4.0, None, ALU.mult)
                        v.wait_ge(xtra_sb, lv * (2 * NPG) + (2 * g + 1))
                        for h in range(2):
                            hs = slice(h * D, (h + 1) * D)
                            last = nc.vector.tensor_copy(bdb[hs, qs, hs], sc[hs, qs, 0, :])
                        last.then_inc(xtra_sb, 1)
                v.wait_ge(xtra_sb, 2 * NPG * EXTRA)
            nc.vector.scalar_tensor_tensor(out=em[:, :, :], in0=sc[:, :, 1, :], scalar=-0.5, in1=sc[:, :, 0, :],
                                           op0=ALU.mult, op1=ALU.add).then_inc(em_sb, 1)
            v.wait_ge(f_mm, 1)
            for h in range(2):
                f_copy(nc.vector.tensor_copy, 0, h).then_inc(f_sb, 1)

            for g in range(NG + 1):
                if g < NG:
                    v.wait_ge(w_hi, g + 1)
                    nc.vector.tensor_tensor(wst[D:128, g % 2, :], py[g % 2][D:128, :], wst[D:128, g % 2, :].bitcast(F32),
                                            ALU.subtract).then_inc(w_lo, 1)
                if g >= 1:
                    for c in range(2):
                        v.wait_ge(o_mm, 3 * (g - 1) + c + 1)
                        nc.vector.tensor_tensor(x[:, g - 1, c, :], pe_[c][0:KC, :], x[:, g - 1, c, :], ALU.add).then_inc(o_dve, 1)

        @block.tensor
        def _(pe):
            pe.wait_ge(p_in, 16)
            for c in range(NC):
                last = nc.tensor.matmul(pq[0][0:D, 0:D], pcs[:, c, :], pcs[:, c, :], start=(c == 0), stop=(c == NC - 1))
            last.then_inc(g_ps, 1)

            def y_mm_(g, r, c, wait_bank=True):
                if c == 0:
                    pe.wait_ge(x_in[r], 16 * (g // 2 + 1) if isinstance(g, int) else g * 8 + (16 - 8 * r))
                    if wait_bank:
                        pe.wait_ge(y_sb, g - 1)
                rhs = x[:, bass.ds(g, 1), c, :] if not isinstance(g, int) else x[:, g, c, :]
                ins = nc.tensor.matmul(py[r][0:D, :], pcs[:, c, :], rhs, start=(c == 0), stop=(c == NC - 1))
                if c == NC - 1:
                    ins.then_inc(y_mm, 1)

            def filler(seq):
                it = iter(seq)
                return lambda: next(it)()

            def block_fill(g, r, wait_bank=True):
                return filler([(lambda c=c: y_mm_(g, r, c, wait_bank)) for c in range(NC)])

            pe.wait_ge(masks, 7)
            newton_pe(pe, qr_mm, qr_sb, 1, block_fill(0, 0, False))
            newton_pe(pe, qr_mm, qr_sb, 4, block_fill(1, 1, False))
            with pe.Fori(1, NEWTON // 2) as i:
                for r in range(2):
                    newton_pe(pe, qr_mm, qr_sb, i * 6 + (3 * r + 1), block_fill(i * 2 + r, r))
            pe.wait_ge(pt_in, 16)
            k = 3 * NEWTON + 1
            pe.wait_ge(qr_sb, k)
            q1_pe(qr_mm)
            with pe.Fori(0, SWEEPS // 3) as i:
                fills = [(lambda g=i * 2 + (NEWTON + r), r=r, c=c: y_mm_(g, r, c)) for r in range(2) for c in range(NC)]
                for j in range(3):
                    sweep_pe(pe, qr_mm, qr_sb, i * 3 + (k + 1 + j))
                    fills[2 * j]()
                    fills[2 * j + 1]()
            k += SWEEPS + 1
            sweep_pe(pe, qr_mm, qr_sb, k)
            g0 = NEWTON + 2 * (SWEEPS // 3)
            for g in range(g0, NG):
                for c in range(NC):
                    y_mm_(g, g % 2, c)
            pe.wait_ge(st_sb, 1)
            for j in range(3):
                last = nc.tensor.matmul(pq[1][0:1, j * D:(j + 1) * D], stats[:, j:j + 1], ident[0:D, 0:D], start=True, stop=True)
            last.then_inc(st_mm, 1)
            pe.wait_ge(flags, 1)
            redo = pe.value_load(redo_qr[0:1, 0:1], min_val=0, max_val=1)
            with pe.If(redo):
                general_pe(pe)
            pe.wait_ge(final, 1)
            nc.tensor.matmul(pq[1][:, 0:N], xd[:, :, :].rearrange("p k d -> p (k d)"), pts[:, :],
                             start=True, stop=True).then_inc(uu_mm, 1)

            pe.wait_ge(silu_done, 1)
            pe.wait_ge(b_in, 16)
            for i in range(HALF_I):
                if i % (HALF_I // 4) == 0:
                    pe.wait_ge(w_in[i // (HALF_I // 4)], 16)
                for c in range(NC):
                    kc = KC + 1 if c == 0 else KC
                    last = nc.tensor.matmul(pe_[i // 16][:, (i % 16) * NB:(i % 16 + 1) * NB], wsym[0:kc, c, i, :],
                                            silu[0:kc, c, :], start=(c == 0), stop=(c == NC - 1))
                if i % 16 == 15:
                    last.then_inc(v_mm, 1)
            pe.wait_ge(fro_sb, 1)
            nc.tensor.matmul(pe_[2][:, 0:NQ], halfm[:, :], fro[:, :], start=True, stop=True).then_inc(fro_mm, 1)
            pe.wait_ge(over_sb, 1)
            nc.tensor.matmul(pe_[3][:, 0:NQ], onesm[:, :], over[:, :], start=True, stop=True).then_inc(cnt_mm, 1)

            pe.wait_ge(bd0, 1)
            for k, (left, right) in enumerate(((bdb, bm), (bdz, z))):
                for g in range(NPG):
                    if k:
                        pe.wait_ge(ex_act, g + 1)
                        pe.wait_ge(ex_dve, g + 1)
                    for q in range(PG):
                        last = nc.tensor.matmul(pe_[g][:, q * D:(q + 1) * D], left[:, g * PG + q, :], right[:, g * PG + q, :],
                                                start=True, stop=True)
                    last.then_inc(ex_mm, 1)

            def products(g, semaphore):
                for q in range(PG):
                    p = g * PG + q
                    last = nc.tensor.matmul(pe_[g][:, q * 2 * D:(q + 1) * 2 * D], semaphore[1][:, p, :],
                                            sc[:, p, :, :].rearrange("p k d -> p (k d)"), start=True, stop=True)
                last.then_inc(semaphore[0], 1)

            for g in range(NPG):
                pe.wait_ge(ex_act, NPG + g + 1)
                pe.wait_ge(ex_dve, NPG + g + 1)
                products(g, (ex_mm, bdz2))
            for g in range(NPG):
                pe.wait_ge(ex_dve, 2 * NPG + g + 1)
                for q in range(PG):
                    nc.tensor.matmul(pe_[g][:, q * D:(q + 1) * D], bdb[:, g * PG + q, :], sc[:, g * PG + q, 1, :], start=True, stop=True)
                for q in range(PG):
                    last = nc.tensor.matmul(pe_[g][:, (PG + q) * D:(PG + q + 1) * D], bdz[:, g * PG + q, :], sc[:, g * PG + q, 0, :],
                                            start=True, stop=True)
                last.then_inc(ex_mm, 1)
            for g in range(NPG):
                pe.wait_ge(ex_act, 2 * NPG + g + 1)
                products(g, (ex_mm, bdb))
            with pe.Fori(1, LEVELS) as lv:
                for g in range(NPG):
                    pe.wait_ge(ex_act, lv * NPG + (2 * NPG + g + 1))
                    pe.wait_ge(ex_pool, lv * NPG + (g + 1 - NPG))
                    products(g, (ex_mm, bdb))
            pe.wait_ge(ex_pool, NPG * LEVELS)
            pe.wait_ge(ex_act, (3 + LEVELS) * NPG)
            pe.wait_ge(flags, 2)
            deeper = pe.value_load(more[0:1, 0:1], min_val=0, max_val=1)
            with pe.If(deeper):
                for g in range(NPG):
                    products(g, (xtra_mm, bdb))
                with pe.Fori(1, EXTRA) as lv:
                    for g in range(NPG):
                        pe.wait_ge(xtra_sb, lv * (2 * NPG) + (2 * g + 2 - 2 * NPG))
                        products(g, (xtra_mm, bdb))
            pe.wait_ge(final, 6)
            pe.wait_ge(em_sb, 1)
            for k in range(2):
                nc.tensor.matmul(pe_[k][:, :], bdx[:, :], em[:, k * 8:(k + 1) * 8, :].rearrange("p q d -> p (q d)"),
                                 start=True, stop=True).then_inc(f_mm, 1)

            pe.wait_ge(f_sb, 4)
            pe.wait_ge(y_sb, NG)
            pe.wait_ge(uu_sb, 2)
            for g in range(NG + 1):
                if g < NG:
                    if g >= 2:
                        pe.wait_ge(w_lo, g - 1)
                    for r in range(GB):
                        b = g * GB + r
                        last = nc.tensor.matmul(py[g % 2][:, r * T:(r + 1) * T],
                                                fs[:, b, :, :].rearrange("p k d -> p (k d)"),
                                                y[:, b, :], start=True, stop=True)
                    last.then_inc(w_mm, 1)
                if g >= 1:
                    k = g - 1
                    pe.wait_ge(w_lo, k + 1)
                    for c in range(NC):
                        bank = pe_[c] if c < 2 else pe_[2 + k % 2]
                        if c < 2 and k >= 1:
                            pe.wait_ge(o_dve, 2 * (k - 1) + c + 1)
                        if c == 2 and k >= 2:
                            pe.wait_ge(o_act, k - 1)
                        for j, uu in enumerate((uuh, uul)):
                            last = nc.tensor.matmul(bank[0:KC, :], uu[:, c * KC:(c + 1) * KC], wst[:, k % 2, :],
                                                    start=(j == 0), stop=(j == 1))
                        last.then_inc(o_mm, 1)


def kernel(x, cond_1152, L0_cond_P, L0_cond_W, L0_cond_b):
    import numpy as np
    import concourse.bacc as bacc
    from concourse.bass_utils import run_bass_kernel_spmd

    xb = np.ascontiguousarray(np.asarray(x).reshape(NG, BT, NC, KC).transpose(0, 3, 2, 1))
    cond = np.ascontiguousarray(np.asarray(cond_1152).reshape(NB, NC, KC).transpose(2, 1, 0))
    P = np.asarray(L0_cond_P)
    pc = np.ascontiguousarray(P.reshape(NC, KC, D).transpose(1, 0, 2))
    pt = np.ascontiguousarray(P.T)
    iu, ju = np.triu_indices(D, k=1)
    where = np.zeros((D, D), np.int64)
    where[iu, ju] = where[ju, iu] = np.arange(len(iu))
    where = where.reshape(2, HALF_I, D).transpose(1, 0, 2).reshape(HALF_I, 2 * D)
    W = np.asarray(L0_cond_W)
    wd = np.ascontiguousarray(W[where].reshape(HALF_I, 2 * D, NC, KC).transpose(3, 2, 0, 1))
    bd = np.ascontiguousarray(np.asarray(L0_cond_b)[where][None])

    nc = bacc.Bacc("TRN2", target_bir_lowering=False, num_devices=1)
    arrays = {"xb": xb, "cond": cond, "pc": pc, "pt": pt, "wd": wd, "bd": bd}
    args = [nc.dram_tensor(k, a.shape, mybir.dt.from_np(a.dtype), kind="ExternalInput").ap() for k, a in arrays.items()]
    out = nc.dram_tensor("out", xb.shape, F32, kind="ExternalOutput").ap()
    rotation_kernel(nc, *args, out)
    r = run_bass_kernel_spmd(nc, [arrays], core_ids=[0])
    got = r.results[0]["out"]
    return np.ascontiguousarray(got.transpose(0, 3, 2, 1)).reshape(NB, T, N)
```

```python
from contextlib import ExitStack

import concourse.bass as bass
from concourse import mybir

F32 = mybir.dt.float32
F32R = mybir.dt.float32r
I32 = mybir.dt.int32
ALU = mybir.AluOpType
ACT = mybir.ActivationFunctionType
AX = mybir.AxisListType

NB = 32
T = 256
N = 288
D = 64
NC = 3
KC = N // NC
GB = 2
NG = NB // GB
BT = GB * T
NQ = NB // 2
PG = 4
NPG = NQ // PG
Q = 32
JH = Q // 2

LEVELS = 3
EXTRA = 10
NORM_LIMIT = 21.0
NEWTON = 6
SWEEPS = 12
GENERAL_NEWTON = 24
NEWTON_TOL = 1e-4
SIGN_MARGIN = 256.0

C2, C3, C4, C5, C6 = 0.0416666571657677, 0.00138887393400706, 2.479333172713527e-05, 2.734932968796656e-07, 1.8413557053625046e-09
S1, S2, S3, S4, S5 = 0.166666591359001, 0.008333188068671657, 0.00019832099913381806, 2.7302947877662567e-06, 2.1809401449776777e-08


def rotation_kernel(nc, xb, cond, pc, pt, wd, bd, out):
    with ExitStack() as ctx:
        def sb(name, shape, dt=F32):
            return ctx.enter_context(nc.sbuf_tensor(name, shape, dt))

        def sem(name):
            return ctx.enter_context(nc.semaphore(name))

        x = sb("x", [KC, NG, NC, BT])
        def at_room(*tensors):
            with ExitStack() as room:
                return [room.enter_context(nc.sbuf_tensor(name, shape, dt)) for name, shape, dt in tensors]

        wq, xs = at_room(("wq", [KC + 1, NC, JH, 4 * Q], F32), ("xs", [KC, 2, NC, 2, BT], F32R))
        pair = [128, NQ, 2, D]
        bdz, bdz2, zz, r1, sc, zb = at_room(
            ("bdz", [128, NQ, 128], F32), ("bdz2", [128, NQ, 128], F32),
            ("zz", pair, F32), ("r1", pair, F32), ("sc", pair, F32), ("zb", pair, F32))
        zz_flat, r1_flat = (t[:, :, :, :].rearrange("p q k d -> p (q k d)") for t in (zz, r1))
        v1, v2, tri1, tri2 = (zz_flat[:, k:k + 512].rearrange("p (q j) -> p q j", q=NQ) for k in range(0, 2048, 512))
        tri3, tri4 = (r1_flat[:, k:k + 512].rearrange("p (q j) -> p q j", q=NQ) for k in range(0, 1024, 512))
        fh, em, tmp, fl, ys = at_room(
            ("fh", [128, NB, 2, D], F32R), ("em", [128, NQ, D], F32), ("tmp", [KC, 2, BT], F32),
            ("fl", [128, NB, 2, D], F32R), ("ys", [128, 2, 2, BT], F32R))
        room = sb("room", [128, 12288])
        y = sb("y", [128, NG, BT])
        pcs = sb("pcs", [KC, NC, D])
        phl = sb("phl", [KC, NC, 2, D], F32R)
        pts = sb("pts", [D, N])
        cnd = sb("cnd", [KC, NC, NB])
        cexp = sb("cexp", [KC, NC, NB])
        silu = sb("silu", [KC + 1, NC, NB])
        ident = sb("ident", [128, 128])
        neg3 = sb("neg3", [D, D])
        pos2 = sb("pos2", [D, D])
        phi = sb("phi", [D, D])
        su = sb("su", [D, D])
        suh = sb("suh", [D, D])
        colm = sb("colm", [D, 2 * D])
        onesm = sb("onesm", [128, 128])
        upm = sb("upm", [128, Q])
        lom = sb("lom", [128, Q])
        ups = sb("ups", [128, Q])
        los = sb("los", [128, Q])
        gs = sb("gs", [D, 2 * D])
        xx = sb("xx", [D, 2 * D])
        tm = sb("tm", [D, D])
        mm = sb("mm", [D, 2 * D])
        junk = sb("junk", [D, 2 * D])
        small = sb("small", [D, 8])
        qq = sb("qq", [D, 2 * D])
        qh = sb("qh", [D, 1])
        cc = sb("cc", [D, 2 * D])
        cl = sb("cl", [D, 2 * D])
        ul = sb("ul", [D, 2 * D])
        ul2 = sb("ul2", [D, 2 * D])
        hp = sb("hp", [D, 1])
        uh = sb("uh", [D, 1])
        ur = sb("ur", [D, 1])
        stats = sb("stats", [D, 4])
        st1 = sb("st1", [1, 8])
        redo_qr = sb("redo_qr", [1, 1], I32)
        phij = sb("phij", [D, D])
        inact = sb("inact", [D, D])
        sg = sb("sg", [128, 1])
        xd = sb("xd", [D, 2, D])
        bdx = sb("bdx", [128, 128])
        uuh = sb("uuh", [128, N], F32R)
        uul = sb("uul", [128, N], F32R)
        vsq = sb("vsq", [128, JH, NB])
        vss = sb("vss", [128, NB])
        cnt = sb("cnt", [128, 1])
        nfac = sb("nfac", [128, 1])
        fac = sb("fac", [128, 1])
        more = sb("more", [1, 1], I32)
        bdb = sb("bdb", [128, NQ, 128])
        wst = sb("wst", [128, 2, BT], F32R)

        ps = [ctx.enter_context(nc.psum_tensor(f"ps{i}", [128, 512], F32)) for i in range(8)]
        pq = ps[0:2]
        py = ps[2:4]
        pe_ = ps[4:8]

        p_in, pt_in, c_in = sem("p_in"), sem("pt_in"), sem("c_in")
        w_in = [sem(f"w_in{i}") for i in range(4)]
        b_in = sem("b_in")
        x_in = [sem("x_in0"), sem("x_in1")]
        masks = sem("masks")
        pool_chain = sem("pool_chain")
        ones_row = sem("ones_row")
        exp_done, silu_done = sem("exp_done"), sem("silu_done")
        dv = sem("dv")
        g_ps, gdiag, groot = sem("g_ps"), sem("gdiag"), sem("groot")
        qr_mm, qr_sb = sem("qr_mm"), sem("qr_sb")
        y_mm, y_sb = sem("y_mm"), sem("y_sb")
        v_mm, b_sb = sem("v_mm"), sem("b_sb")
        vsq_done, vss_sb, vss_mm, v1_sb, v2_sb = sem("vsq_done"), sem("vss_sb"), sem("vss_mm"), sem("v1_sb"), sem("v2_sb")
        fac_sb = sem("fac_sb")
        p_hi, p_lo, x_hi, x_lo_pool, x_lo_dve = sem("p_hi"), sem("p_lo"), sem("x_hi"), sem("x_lo_pool"), sem("x_lo_dve")
        bd0, bdz_clear = sem("bd0"), sem("bdz_clear")
        flags = sem("flags")
        st_mm, st_sb = sem("st_mm"), sem("st_sb")
        ex_mm = sem("ex_mm")
        ex_act, ex_dve, ex_pool = sem("ex_act"), sem("ex_dve"), sem("ex_pool")
        gen_mm, gen_sb, gen_dv = sem("gen_mm"), sem("gen_sb"), sem("gen_dv")
        xtra_mm, xtra_sb = sem("xtra_mm"), sem("xtra_sb")
        final = sem("final")
        uu_mm, uu_sb = sem("uu_mm"), sem("uu_sb")
        em_sb, f_mm, f_hi, f_lo = sem("em_sb"), sem("f_mm"), sem("f_hi"), sem("f_lo")
        y_hi, y_lo_dve, y_lo_pool = sem("y_hi"), sem("y_lo_dve"), sem("y_lo_pool")
        w_mm, w_hi, w_lo = sem("w_mm"), sem("w_hi"), sem("w_lo")
        o_mm, o_dve, o_act, o_pool = sem("o_mm"), sem("o_dve"), sem("o_act"), sem("o_pool")
        stored = sem("stored")

        block = ctx.enter_context(nc.Block())

        @block.sync
        def _(sp):
            sp.dma_start(pcs[:, :, :], pc).then_inc(p_in, 16)
            sp.dma_start(pts[:, :], pt).then_inc(pt_in, 16)
            sp.dma_start(cnd[:, :, :], cond).then_inc(c_in, 16)
            sp.dma_start(x[:, 0, :, :], xb[0, :, :, :]).then_inc(x_in[0], 16)
            sp.dma_start(x[:, 1, :, :], xb[1, :, :, :]).then_inc(x_in[1], 16)
            sp.dma_start(wq[KC:KC + 1, 0, :, :], bd).then_inc(b_in, 16)

            WQ = JH // 4
            for k in range(4):
                for r in range(2):
                    g = 2 + 2 * k + r
                    sp.wait_ge(x_in[r], 16 * (k + 1))
                    sp.dma_start(x[:, g, :, :], xb[g, :, :, :]).then_inc(x_in[r], 16)
                sp.dma_start(wq[0:KC, :, k * WQ:(k + 1) * WQ, :], wd[:, :, k * WQ:(k + 1) * WQ, :]).then_inc(w_in[k], 16)
            for k in range(4, NG // 2 - 1):
                for r in range(2):
                    g = 2 + 2 * k + r
                    sp.wait_ge(x_in[r], 16 * (k + 1))
                    sp.dma_start(x[:, g, :, :], xb[g, :, :, :]).then_inc(x_in[r], 16)

            for g in range(NG):
                sp.wait_ge(o_dve, 2 * g + 2)
                sp.wait_ge(o_pool, g + 1)
                sp.dma_start(out[g, :, :, :], x[:, g, :, :]).then_inc(stored, 16)
            sp.wait_ge(stored, 16 * NG)

        @block.gpsimd
        def _(pool):
            n = [0]

            def link(ins):
                n[0] += 1
                ins.then_inc(pool_chain, 1)
                pool.wait_ge(pool_chain, n[0])

            link(nc.gpsimd.memset(mm[:, D:2 * D], 0.0))
            link(nc.gpsimd.memset(ident[:, :], 0.0))
            nc.gpsimd.affine_select(out=ident[:, :], in_=ident[:, :], compare_op=ALU.not_equal, fill=1.0,
                                    base=0, pattern=[[-1, 128]], channel_multiplier=1).then_inc(masks, 1)
            for dst, val in ((neg3, -3.0), (pos2, 2.0)):
                link(nc.gpsimd.memset(dst[:, :], 0.0))
                nc.gpsimd.affine_select(out=dst[:, :], in_=dst[:, :], compare_op=ALU.not_equal, fill=val,
                                        base=0, pattern=[[-1, D]], channel_multiplier=1).then_inc(masks, 1)
            for dst, val in ((phi, -1.0), (su, 1.0), (suh, 0.5)):
                link(nc.gpsimd.memset(dst[:, :], val))
                last = nc.gpsimd.affine_select(out=dst[:, :], in_=dst[:, :], compare_op=ALU.is_gt, fill=0.0,
                                               base=0, pattern=[[1, D]], channel_multiplier=-1)
                if dst is phi:
                    link(last)
                    last = nc.gpsimd.affine_select(out=dst[:, :], in_=dst[:, :], compare_op=ALU.not_equal, fill=-0.5,
                                                   base=0, pattern=[[-1, D]], channel_multiplier=1)
                last.then_inc(masks, 1)
            for dst, sign in ((upm, 1), (lom, -1)):
                link(nc.gpsimd.memset(dst[:, :], 1.0))
                for k in range(4):
                    rows = dst[k * Q:(k + 1) * Q, :]
                    link(nc.gpsimd.affine_select(out=rows, in_=rows, compare_op=ALU.is_gt, fill=0.0,
                                                 base=0, pattern=[[sign, Q]], channel_multiplier=-sign))
            link(nc.gpsimd.memset(colm[:, 0:D], 1.0))
            link(nc.gpsimd.memset(colm[:, D:2 * D], 0.0))
            link(nc.gpsimd.memset(onesm[:, :], 1.0))
            nc.gpsimd.memset(silu[KC:KC + 1, :, :], 1.0).then_inc(masks, 1)

            with pool.Fori(0, NG // 2) as h:
                for r in range(2):
                    pool.wait_ge(x_hi, h * 2 + (r + 1))
                    nc.gpsimd.tensor_tensor(xs[:, r, 0:2, 1, :], x[:, bass.ds(h * 2 + r, 1), 0:2, :].rearrange("p a c t -> p (a c) t"),
                                            xs[:, r, 0:2, 0, :].bitcast(F32), ALU.subtract).then_inc(x_lo_pool, 1)
            nc.gpsimd.memset(bdb[:, :, :], 0.0).then_inc(bdz_clear, 1)
            pool.wait_ge(v_mm, 1)
            nc.gpsimd.memset(bdz[:, :, :], 0.0)
            nc.gpsimd.memset(bdz2[:, :, :], 0.0).then_inc(bdz_clear, 1)

            with pool.Fori(0, LEVELS + 1) as lv:
                for g in range(NPG):
                    qs = slice(g * PG, (g + 1) * PG)
                    pool.wait_ge(ex_dve, lv * NPG + (3 * NPG + g + 1))
                    nc.gpsimd.tensor_tensor(bdb[0:D, qs, 0:D], sc[0:D, qs, 1, :],
                                            onesm[0:D, 0:D].rearrange("p (a d) -> p a d", a=1).to_broadcast([D, PG, D]),
                                            ALU.mult).then_inc(ex_pool, 1)

            for g in range(-1, NG):
                if g % 2 == 0 and g + 1 < NG:
                    pool.wait_ge(y_hi, g + 2)
                    nc.gpsimd.tensor_tensor(ys[:, 1, 1, :], y[:, g + 1, :], ys[:, 1, 0, :].bitcast(F32),
                                            ALU.subtract).then_inc(y_lo_pool, 1)
                if g >= 1:
                    k = g - 1
                    pool.wait_ge(o_act, k + 1)
                    nc.gpsimd.tensor_tensor(x[:, k, 2, :], x[:, k, 2, :], tmp[:, k % 2, :], ALU.add).then_inc(o_pool, 1)
            pool.wait_ge(o_act, NG)
            nc.gpsimd.tensor_tensor(x[:, NG - 1, 2, :], x[:, NG - 1, 2, :], tmp[:, (NG - 1) % 2, :], ALU.add).then_inc(o_pool, 1)

        def f_twice(k):
            return pq[k % 2][:, :].rearrange("p (b a d) -> p b a d", b=8, a=1).to_broadcast([128, 8, 2, D])

        @block.scalar
        def _(act):
            act.wait_ge(c_in, 16)
            nc.scalar.activation(cexp[:, :, :], cnd[:, :, :], ACT.Exp, scale=-1.0).then_inc(exp_done, 1)
            act.wait_ge(gdiag, 1)
            nc.scalar.activation(small[:, 1:2], small[:, 0:1], ACT.Sqrt).then_inc(groot, 1)

            act.wait_ge(p_in, 16)
            nc.scalar.activation(phl[:, :, 0, :], pcs[:, :, :], ACT.Copy).then_inc(p_hi, 1)
            for r in range(2):
                act.wait_ge(x_in[r], 16)
                nc.scalar.activation(xs[:, r, :, 0, :], x[:, r, :, :], ACT.Copy).then_inc(x_hi, 1)
            with act.Fori(0, NG // 2 - 1) as h:
                for r in range(2):
                    act.wait_ge(y_mm, h * 2 + (r + 1))
                    nc.scalar.activation(y[:, bass.ds(h * 2 + r, 1), :].rearrange("p a t -> p (a t)"),
                                         py[r][:, :], ACT.Copy).then_inc(y_sb, 1)
                    act.wait_ge(x_in[r], h * 16 + 32)
                    nc.scalar.activation(xs[:, r, :, 0, :], x[:, bass.ds(h * 2 + (2 + r), 1), :, :].rearrange("p a c t -> p (a c) t"),
                                         ACT.Copy).then_inc(x_hi, 1)
            for g in (NG - 2, NG - 1):
                act.wait_ge(y_mm, g + 1)
                nc.scalar.activation(y[:, g, :], py[g % 2][:, :], ACT.Copy).then_inc(y_sb, 1)

            act.wait_ge(v_mm, 1)
            nc.scalar.activation(vsq[:, :, :].rearrange("p j b -> p (j b)"), pe_[0][:, :], ACT.Square).then_inc(vsq_done, 1)
            act.wait_ge(fac_sb, 1)
            act.wait_ge(v1_sb, 4)
            for h in range(2):
                nc.scalar.activation(zb[h * D:h * D + Q, :, 1, Q:D], v1[h * D + Q:(h + 1) * D, :, :], ACT.Copy,
                                     scale=fac[h * D + Q:(h + 1) * D, 0:1]).then_inc(b_sb, 1)
            act.wait_ge(v2_sb, 1)
            for h in range(2):
                nc.scalar.activation(zb[h * D + Q:(h + 1) * D, :, 1, 0:Q], v2[h * D + Q:(h + 1) * D, :, :], ACT.Copy,
                                     scale=nfac[h * D + Q:(h + 1) * D, 0:1]).then_inc(b_sb, 1)

            for g in range(NPG):
                qs = slice(g * PG, (g + 1) * PG)
                act.wait_ge(ex_mm, g + 1)
                nc.scalar.activation(zb[:, qs, 0, :], pe_[g][:, 0:PG * D].rearrange("p (q d) -> p q d", q=PG),
                                     ACT.Copy, scale=-1.0).then_inc(ex_act, 1)
            for g in range(NPG):
                act.wait_ge(ex_mm, NPG + g + 1)
                nc.scalar.activation(zz[:, g * PG:(g + 1) * PG, :, :].rearrange("p q k d -> p (q k d)"), pe_[g][:, :],
                                     ACT.Copy).then_inc(ex_act, 1)
            for g in range(NPG):
                qs = slice(g * PG, (g + 1) * PG)
                act.wait_ge(ex_dve, 3 * NPG + g + 1)
                nc.scalar.activation(bdb[D:128, qs, D:128], sc[D:128, qs, 1, :], ACT.Copy).then_inc(ex_act, 1)
            with act.Fori(0, LEVELS) as lv:
                for g in range(NPG):
                    qs = slice(g * PG, (g + 1) * PG)
                    pg = pe_[g][:, :].rearrange("p (q k d) -> p q k d", q=PG, k=2)
                    act.wait_ge(ex_dve, lv * NPG + (4 * NPG + g + 1))
                    nc.scalar.activation(bdb[D:128, qs, D:128], sc[D:128, qs, 1, :], ACT.Copy)
                    nc.scalar.activation(sc[:, qs, 0, :], pg[:, :, 1, :], ACT.Copy, scale=4.0).then_inc(ex_act, 1)

            def y_high(g):
                if g >= 2:
                    act.wait_ge(w_mm, g - 1)
                nc.scalar.activation(ys[:, g % 2, 0, :], y[:, g, :], ACT.Copy).then_inc(y_hi, 1)

            act.wait_ge(em_sb, 1)
            y_high(0)
            def f_high(k):
                act.wait_ge(f_mm, k + 1)
                nc.scalar.activation(fh[:, k * 8:(k + 1) * 8, :, :], f_twice(k), ACT.Copy).then_inc(f_hi, 1)

            f_high(0)
            f_high(1)
            for g in range(NG + 1):
                if g + 1 < NG:
                    y_high(g + 1)
                if g < NG:
                    act.wait_ge(w_mm, g + 1)
                    if g >= 2:
                        act.wait_ge(o_mm, 3 * (g - 1))
                    nc.scalar.activation(wst[:, g % 2, :], py[g % 2][:, :], ACT.Copy).then_inc(w_hi, 1)
                if g in (1, 2):
                    f_high(g + 1)
                if g >= 1:
                    k = g - 1
                    act.wait_ge(o_mm, 3 * k + 3)
                    if k >= 2:
                        act.wait_ge(o_pool, k - 1)
                    nc.scalar.activation(tmp[:, k % 2, :], pe_[2 + k % 2][0:KC, :], ACT.Copy).then_inc(o_act, 1)

        def newton_dve(v, mmsem, sbsem, k, active=None, check=False):
            v.wait_ge(mmsem, k + 1)
            nc.vector.tensor_copy(tm[:, :], pq[0][0:D, 0:D]).then_inc(sbsem, 1)
            v.wait_ge(mmsem, k + 2)
            if active is None:
                nc.vector.tensor_tensor(mm[:, 0:D], pq[1][0:D, 0:D], phi[:, :], ALU.mult).then_inc(sbsem, 1)
            else:
                v.wait_ge(gen_dv, active - 1)
                nc.vector.tensor_tensor(junk[:, 0:D], pq[1][0:D, 0:D], phij[:, :], ALU.mult).then_inc(gen_dv, 1)
                v.wait_ge(gen_dv, active)
                nc.vector.tensor_tensor(mm[:, 0:D], junk[:, 0:D], inact[:, :], ALU.add).then_inc(sbsem, 1)
            if check:
                nc.vector.tensor_tensor(junk[:, 0:D], pq[1][0:D, 0:D], pos2[:, :], ALU.add).then_inc(gdiag, 1)
            v.wait_ge(mmsem, k + 3)
            nc.vector.tensor_copy(xx[:, :], pq[0][0:D, 0:2 * D]).then_inc(sbsem, 1)

        def newton_pe(pe, mmsem, sbsem, k, filler=None):
            f = filler or (lambda: None)
            pe.wait_ge(sbsem, k)
            nc.tensor.matmul(pq[0][:, 0:D], gs[:, :], xx[:, 0:D], start=True, stop=True).then_inc(mmsem, 1)
            nc.tensor.matmul(pq[1][:, 0:D], ident[0:D, :], neg3[:, :], start=True, stop=False)
            f()
            pe.wait_ge(sbsem, k + 1)
            nc.tensor.matmul(pq[1][:, 0:D], xx[:, :], tm[:, :], start=False, stop=True).then_inc(mmsem, 1)
            f()
            pe.wait_ge(sbsem, k + 2)
            nc.tensor.matmul(pq[0][:, D:2 * D], mm[:, :], xx[:, D:2 * D], start=True, stop=True)
            nc.tensor.matmul(pq[0][0:D, 0:D], xx[:, D:2 * D], mm[:, 0:D], start=True, stop=True).then_inc(mmsem, 1)
            f()

        def q1_pe(mmsem):
            nc.tensor.matmul(pq[1][0:D, 0:D], pts[:, 0:D], xx[:, 0:D], start=True, stop=True)
            nc.tensor.matmul(pq[1][0:D, D:2 * D], xx[:, 0:D], pts[:, 0:D], start=True, stop=True).then_inc(mmsem, 1)

        def q1_dve(v, mmsem, k, sbsem, dvsem, base):
            v.wait_ge(mmsem, k)
            nc.vector.tensor_copy(qq[:, :], pq[1][0:D, 0:2 * D]).then_inc(dvsem, 1)
            v.wait_ge(dvsem, base + 1)
            nc.vector.tensor_tensor_reduce(out=junk[:, 0:D], in0=qq[:, 0:D], in1=ident[0:D, 0:D], scale=0.5, scalar=-0.5,
                                           op0=ALU.mult, op1=ALU.add, accum_out=qh[:, 0:1]).then_inc(dvsem, 1)
            v.wait_ge(dvsem, base + 2)
            nc.vector.memset(ul[:, :], 0.0).then_inc(sbsem, 1)

        def sweep_pe(pe, mmsem, sbsem, k):
            pe.wait_ge(sbsem, k)
            nc.tensor.matmul(pq[0][:, D:2 * D], ul[:, :], ul[:, D:2 * D], start=True, stop=True)
            nc.tensor.matmul(pq[0][0:D, 0:D], ul[:, D:2 * D], ul[:, 0:D], start=True, stop=True).then_inc(mmsem, 1)

        def x_low(v, g, r):
            v.wait_ge(x_hi, g + 1)
            src = x[:, g, 2, :] if isinstance(g, int) else x[:, bass.ds(g, 1), 2, :].rearrange("p a t -> p (a t)")
            nc.vector.tensor_tensor(xs[:, r, 2, 1, :], src, xs[:, r, 2, 0, :].bitcast(F32), ALU.subtract).then_inc(x_lo_dve, 1)

        SWEEP_DV = 5

        def sweep_dve(v, mmsem, k, sbsem, dvsem, base, dst):
            v.wait_ge(mmsem, k)
            nc.vector.tensor_tensor_reduce(out=junk[:, 0:D], in0=pq[0][0:D, 0:D], in1=ident[0:D, 0:D],
                                           scale=-0.5, scalar=qh[:, 0:1], op0=ALU.mult, op1=ALU.add,
                                           accum_out=hp[:, 0:1]).then_inc(dvsem, 1)
            nc.vector.tensor_tensor(cc[:, :], qq[:, :], pq[0][0:D, 0:2 * D], ALU.subtract).then_inc(dvsem, 1)
            v.wait_ge(dvsem, base + 1)
            nc.vector.scalar_tensor_tensor(out=uh[:, :], in0=hp[:, :], scalar=-0.5, in1=hp[:, :],
                                           op0=ALU.is_ge, op1=ALU.add).then_inc(dvsem, 1)
            v.wait_ge(dvsem, base + 2)
            nc.vector.tensor_scalar(cl[:, :], cc[:, :], 4.0, -4.0, ALU.min, ALU.max).then_inc(dvsem, 1)
            v.wait_ge(dvsem, base + 3)
            nc.vector.reciprocal(ur[:, :], uh[:, :]).then_inc(dvsem, 1)
            v.wait_ge(dvsem, base + 4)
            nc.vector.tensor_tensor(dst[:, 0:D], cl[:, 0:D], su[:, :], ALU.mult)
            v.wait_ge(dvsem, base + 5)
            nc.vector.scalar_tensor_tensor(out=dst[:, D:2 * D], in0=cl[:, D:2 * D], scalar=ur[:, 0:1],
                                           in1=suh[:, :], op0=ALU.mult, op1=ALU.mult).then_inc(sbsem, 1)

        GEN_STEPS = D * GENERAL_NEWTON
        GEN_X = 3 * GEN_STEPS + 1

        def general_dve(v):
            for h in range(2):
                last = nc.vector.tensor_scalar(xx[:, h * D:(h + 1) * D], ident[0:D, 0:D], small[:, 2:3], None, ALU.mult)
            last.then_inc(gen_sb, 1)
            with v.Fori(0, D) as j:
                per = GENERAL_NEWTON + 3
                upto = colm[:, bass.ds(D - 1 - j, D)]
                nc.vector.tensor_tensor(phij[:, :], phi[:, :], upto, ALU.mult).then_inc(gen_dv, 1)
                nc.vector.tensor_tensor(junk[:, 0:D], ident[0:D, 0:D], upto, ALU.mult).then_inc(gen_dv, 1)
                v.wait_ge(gen_dv, j * per + 2)
                nc.vector.tensor_tensor(inact[:, :], ident[0:D, 0:D], junk[:, 0:D], ALU.subtract).then_inc(gen_dv, 1)
                with v.Fori(0, GENERAL_NEWTON) as i:
                    newton_dve(v, gen_mm, gen_sb, j * (3 * GENERAL_NEWTON) + i * 3, active=j * per + (i + 4))
            base = D * (GENERAL_NEWTON + 3)
            q1_dve(v, gen_mm, GEN_X, gen_sb, gen_dv, base)
            with v.Fori(0, D) as i:
                sweep_dve(v, gen_mm, i + (GEN_X + 1), gen_sb, gen_dv, i * SWEEP_DV + (base + 2), ul)

        def general_pe(pe):
            with pe.Fori(0, GEN_STEPS) as n:
                newton_pe(pe, gen_mm, gen_sb, n * 3 + 1)
            pe.wait_ge(gen_sb, GEN_X)
            q1_pe(gen_mm)
            with pe.Fori(0, D) as i:
                sweep_pe(pe, gen_mm, gen_sb, i + (GEN_X + 1))

        @block.vector
        def _(v):
            count = [0]

            def out_(ins):
                ins.then_inc(dv, 1)
                count[0] += 1
                return count[0]

            def start_x():
                for h in range(2):
                    last = nc.vector.tensor_scalar(xx[:, h * D:(h + 1) * D], ident[0:D, 0:D], small[:, 2:3], None, ALU.mult)
                return last

            v.wait_ge(masks, 1)
            v.wait_ge(g_ps, 1)
            nc.vector.tensor_tensor_reduce(out=junk[:, 0:D], in0=pq[0][0:D, 0:D], in1=ident[0:D, 0:D],
                                           scale=1.0, scalar=0.0, op0=ALU.mult, op1=ALU.add,
                                           accum_out=small[:, 0:1]).then_inc(gdiag, 1)
            for h in range(2):
                nc.vector.tensor_copy(gs[:, h * D:(h + 1) * D], pq[0][0:D, 0:D])
            v.wait_ge(groot, 1)
            v.wait_ge(dv, out_(nc.vector.reciprocal(small[:, 2:3], small[:, 1:2])))
            start_x().then_inc(qr_sb, 1)

            v.wait_ge(p_hi, 1)
            nc.vector.tensor_tensor(phl[:, :, 1, :], pcs[:, :, :], phl[:, :, 0, :].bitcast(F32), ALU.subtract).then_inc(p_lo, 1)

            v.wait_ge(exp_done, 1)
            v.wait_ge(dv, out_(nc.vector.tensor_scalar(cexp[:, :, :], cexp[:, :, :], 1.0, None, ALU.add)))
            v.wait_ge(dv, out_(nc.vector.reciprocal(cexp[:, :, :], cexp[:, :, :])))
            nc.vector.tensor_tensor(silu[0:KC, :, :], cnd[:, :, :], cexp[:, :, :], ALU.mult).then_inc(silu_done, 1)

            v.wait_ge(masks, 7)
            with v.Fori(0, NEWTON // 2 - 1) as i:
                for r in range(2):
                    newton_dve(v, qr_mm, qr_sb, i * 6 + 3 * r)
                    x_low(v, i * 2 + r, r)
            newton_dve(v, qr_mm, qr_sb, 3 * (NEWTON - 2))
            x_low(v, NEWTON - 2, 0)
            newton_dve(v, qr_mm, qr_sb, 3 * (NEWTON - 1), check=True)
            x_low(v, NEWTON - 1, 1)
            v.wait_ge(gdiag, 2)
            nc.vector.tensor_reduce(stats[:, 0:1], junk[:, 0:D], AX.X, ALU.max, apply_absolute_value=True)
            k = 3 * NEWTON + 1
            q1_dve(v, qr_mm, k, qr_sb, dv, count[0])
            count[0] += 2

            base = count[0]
            with_x = (NG - NEWTON) // 2
            with v.Fori(0, with_x) as i:
                for r in range(2):
                    sweep_dve(v, qr_mm, i * 2 + (k + 1 + r), qr_sb, dv, i * (2 * SWEEP_DV) + (base + r * SWEEP_DV), ul)
                    x_low(v, i * 2 + (NEWTON + r), r)
            with v.Fori(2 * with_x, SWEEPS) as i:
                sweep_dve(v, qr_mm, i + (k + 1), qr_sb, dv, i * SWEEP_DV + base, ul)
            count[0] += SWEEPS * SWEEP_DV
            k += SWEEPS + 1
            sweep_dve(v, qr_mm, k, qr_sb, dv, count[0], ul2)
            count[0] += SWEEP_DV
            v.wait_ge(qr_sb, k + 1)
            v.wait_ge(dv, out_(nc.vector.tensor_tensor(junk[:, :], ul[:, :], ul2[:, :], ALU.subtract)))
            v.wait_ge(dv, out_(nc.vector.tensor_scalar(small[:, 4:5], hp[:, :], 2.0, 1.0, ALU.mult, ALU.add)))
            v.wait_ge(dv, out_(nc.vector.tensor_reduce(small[:, 5:6], junk[:, :], AX.X, ALU.max, apply_absolute_value=True)))
            v.wait_ge(dv, out_(nc.vector.tensor_scalar(stats[:, 1:2], small[:, 5:6], SIGN_MARGIN, None, ALU.mult)))
            nc.vector.tensor_reduce(stats[:, 2:3], small[:, 4:5], AX.X, ALU.max, apply_absolute_value=True, negate=True).then_inc(st_sb, 1)
            v.wait_ge(st_mm, 1)
            v.wait_ge(dv, out_(nc.vector.tensor_reduce(st1[0:1, 0:3], pq[1][0:1, 0:3 * D].rearrange("p (k d) -> p k d", k=3), AX.X, ALU.max)))
            v.wait_ge(dv, out_(nc.vector.tensor_tensor(st1[0:1, 3:4], st1[0:1, 1:2], st1[0:1, 2:3], ALU.add)))
            v.wait_ge(dv, out_(nc.vector.tensor_scalar(st1[0:1, 4:5], st1[0:1, 3:4], 0.0, None, ALU.is_le)))
            v.wait_ge(dv, out_(nc.vector.scalar_tensor_tensor(out=st1[0:1, 5:6], in0=st1[0:1, 0:1], scalar=NEWTON_TOL,
                                                              in1=st1[0:1, 4:5], op0=ALU.is_le, op1=ALU.mult)))
            nc.vector.tensor_scalar(redo_qr[0:1, 0:1], st1[0:1, 5:6], -1.0, 1.0, ALU.mult, ALU.add).then_inc(flags, 1)
            v.wait_ge(flags, 1)
            redo = v.value_load(redo_qr[0:1, 0:1], min_val=0, max_val=1)
            with v.If(redo):
                general_dve(v)
            for h in range(2):
                last = nc.vector.tensor_copy(xd[:, h, :], xx[:, 0:D])
            last.then_inc(final, 1)
            nc.vector.tensor_scalar(sg[0:D, :], uh[:, :], 0.0, -2.0, ALU.is_ge, ALU.mult).then_inc(final, 1)
            nc.vector.tensor_scalar(sg[D:128, :], uh[:, :], 0.0, -2.0, ALU.is_ge, ALU.mult).then_inc(final, 1)
            v.wait_ge(final, 3)
            nc.vector.tensor_scalar(sg[:, :], sg[:, :], 1.0, None, ALU.add).then_inc(final, 1)
            v.wait_ge(final, 4)
            for h in range(2):
                for k in range(2):
                    nc.vector.tensor_scalar(bdx[h * D:(h + 1) * D, k * D:(k + 1) * D], xx[:, D:2 * D], sg[0:D, 0:1], None,
                                            ALU.mult).then_inc(final, 1)
            v.wait_ge(uu_mm, 1)
            nc.vector.tensor_scalar(uuh[:, :], pq[1][:, 0:N], sg[:, 0:1], None, ALU.mult).then_inc(uu_sb, 1)
            v.wait_ge(uu_sb, 1)
            nc.vector.scalar_tensor_tensor(out=uul[:, :], in0=pq[1][:, 0:N], scalar=sg[:, 0:1], in1=uuh[:, :].bitcast(F32),
                                           op0=ALU.mult, op1=ALU.subtract).then_inc(uu_sb, 1)

            v.wait_ge(vsq_done, 1)
            nc.vector.tensor_reduce(vss[:, :], vsq[:, :, :].rearrange("p j b -> p b j"), AX.X, ALU.add).then_inc(vss_sb, 1)
            for jh in range(2):
                for h in range(2):
                    src = pe_[0][jh * D:(jh + 1) * D, :].rearrange("p (j b) -> p b j", j=JH)
                    nc.vector.tensor_copy(v1[h * D:(h + 1) * D, :, jh * JH:(jh + 1) * JH],
                                          src[:, h * NQ:(h + 1) * NQ, :]).then_inc(v1_sb, 1)
            v.wait_ge(v1_sb, 4)
            nc.vector.transpose(v2[:, :, :].rearrange("p q j -> p (q j)"), v1[:, :, :].rearrange("p q j -> p (q j)")).then_inc(v2_sb, 1)
            v.wait_ge(vss_mm, 1)
            v.wait_ge(dv, out_(nc.vector.tensor_reduce(cnt[:, :], pe_[1][:, 0:NB], AX.X, ALU.max)))
            nc.vector.tensor_scalar(more[0:1, 0:1], cnt[0:1, :], NORM_LIMIT ** 2, None, ALU.is_gt).then_inc(flags, 1)
            v.wait_ge(dv, out_(nc.vector.tensor_scalar(fac[:, :], cnt[:, :], NORM_LIMIT ** 2, (2.0 ** -EXTRA - 1.0) * 2.0 ** -LEVELS,
                                                       ALU.is_gt, ALU.mult)))
            v.wait_ge(dv, out_(nc.vector.tensor_scalar(fac[:, :], fac[:, :], 2.0 ** -LEVELS, None, ALU.add)))
            nc.vector.tensor_scalar(nfac[:, :], fac[:, :], -1.0, None, ALU.mult).then_inc(fac_sb, 1)
            nc.vector.tensor_scalar(ups[:, :], upm[:, :], fac[:, 0:1], None, ALU.mult)
            v.wait_ge(dv, out_(nc.vector.tensor_scalar(los[:, :], lom[:, :], fac[:, 0:1], None, ALU.mult)))
            v.wait_ge(v2_sb, 1)
            v.wait_ge(y_mm, NG)
            for dst, src, mask in ((tri1, v1, ups), (tri2, v2, los), (tri3, v2, ups), (tri4, v1, los)):
                last = out_(nc.vector.tensor_tensor(dst[:, :, :], src[:, :, :],
                                                    mask[:, :].rearrange("p (a j) -> p a j", a=1).to_broadcast([128, NQ, Q]), ALU.mult))
            v.wait_ge(dv, last)
            for h in range(2):
                rows, other = slice(h * D, h * D + Q), slice(h * D + Q, (h + 1) * D)
                nc.vector.tensor_tensor(zb[rows, :, 1, 0:Q], tri1[rows, :, :], tri2[rows, :, :], ALU.subtract).then_inc(b_sb, 1)
                nc.vector.tensor_tensor(zb[other, :, 1, Q:D], tri3[rows, :, :], tri4[rows, :, :], ALU.subtract).then_inc(b_sb, 1)
            v.wait_ge(b_sb, 8)
            v.wait_ge(bdz_clear, 1)
            for h in range(2):
                last = nc.vector.tensor_copy(bdb[h * D:(h + 1) * D, :, h * D:(h + 1) * D], zb[h * D:(h + 1) * D, :, 1, :])
            last.then_inc(bd0, 1)

            def diag_from_psum(dst, g, scale):
                qs = slice(g * PG, (g + 1) * PG)
                for h in range(2):
                    last = nc.vector.tensor_scalar(
                        dst[h * D:(h + 1) * D, qs, h * D:(h + 1) * D],
                        pe_[g][h * D:(h + 1) * D, 0:PG * D].rearrange("p (q d) -> p q d", q=PG), scale, None, ALU.mult)
                return last

            v.wait_ge(bdz_clear, 2)
            for g in range(NPG):
                v.wait_ge(ex_act, g + 1)
                diag_from_psum(bdz, g, -1.0).then_inc(ex_dve, 1)
            for g in range(NPG):
                qs = slice(g * PG, (g + 1) * PG)
                v.wait_ge(ex_act, NPG + g + 1)
                for h in range(2):
                    hs = slice(h * D, (h + 1) * D)
                    nc.vector.tensor_copy(bdz2[hs, qs, hs], zz[hs, qs, 0, :])
                for k, ratio in ((0, C6 / C5), (1, S5 / S4)):
                    last = nc.vector.scalar_tensor_tensor(out=r1[:, qs, k, :], in0=zz[:, qs, k, :], scalar=ratio, in1=zb[:, qs, k, :],
                                                          op0=ALU.mult, op1=ALU.add)
                last.then_inc(ex_dve, 1)
            out_(nc.vector.scalar_tensor_tensor(out=sc[:, :, 0, :], in0=zz[:, :, 0, :], scalar=-2 * C2, in1=zb[:, :, 0, :],
                                                op0=ALU.mult, op1=ALU.subtract))
            v.wait_ge(dv, out_(nc.vector.scalar_tensor_tensor(out=sc[:, :, 1, :], in0=zz[:, :, 1, :], scalar=S1, in1=zb[:, :, 1, :],
                                                              op0=ALU.mult, op1=ALU.add)))
            for k, ratio in ((0, C4 / C3), (1, S3 / S2)):
                last = out_(nc.vector.scalar_tensor_tensor(out=zb[:, :, k, :], in0=zz[:, :, k, :], scalar=ratio, in1=zb[:, :, k, :],
                                                           op0=ALU.mult, op1=ALU.add))
            v.wait_ge(dv, last)
            for g in range(NPG):
                qs = slice(g * PG, (g + 1) * PG)
                pg = pe_[g][:, :].rearrange("p (q k d) -> p q k d", q=PG, k=2)
                v.wait_ge(ex_mm, 2 * NPG + g + 1)
                for k, factor in ((0, C5 / C3), (1, S4 / S2)):
                    last = nc.vector.scalar_tensor_tensor(out=zb[:, qs, k, :], in0=pg[:, :, k, :], scalar=factor,
                                                          in1=zb[:, qs, k, :], op0=ALU.mult, op1=ALU.add)
                last.then_inc(ex_dve, 1)
            for g in range(NPG):
                qs = slice(g * PG, (g + 1) * PG)
                pg = pe_[g][:, :].rearrange("p (q k d) -> p q k d", q=PG, k=2)
                v.wait_ge(ex_mm, 3 * NPG + g + 1)
                for k, factor in ((0, -2 * C3), (1, S2)):
                    last = nc.vector.scalar_tensor_tensor(out=sc[:, qs, k, :], in0=pg[:, :, k, :], scalar=factor,
                                                          in1=sc[:, qs, k, :], op0=ALU.mult, op1=ALU.add)
                last.then_inc(ex_dve, 1)
            with v.Fori(0, LEVELS) as lv:
                for g in range(NPG):
                    qs = slice(g * PG, (g + 1) * PG)
                    pg = pe_[g][:, :].rearrange("p (q k d) -> p q k d", q=PG, k=2)
                    v.wait_ge(ex_mm, lv * NPG + (4 * NPG + g + 1))
                    nc.vector.scalar_tensor_tensor(out=sc[:, qs, 1, :], in0=sc[:, qs, 1, :], scalar=2.0, in1=pg[:, :, 0, :],
                                                   op0=ALU.mult, op1=ALU.add).then_inc(ex_dve, 1)
            v.wait_ge(ex_act, (3 + LEVELS) * NPG)
            v.wait_ge(ex_pool, (1 + LEVELS) * NPG)
            v.wait_ge(ex_dve, (4 + LEVELS) * NPG)
            deeper = v.value_load(more[0:1, 0:1], min_val=0, max_val=1)
            with v.If(deeper):
                with v.Fori(0, EXTRA) as lv:
                    for g in range(NPG):
                        qs = slice(g * PG, (g + 1) * PG)
                        pg = pe_[g][:, :].rearrange("p (q k d) -> p q k d", q=PG, k=2)
                        v.wait_ge(xtra_mm, lv * NPG + (g + 1))
                        nc.vector.scalar_tensor_tensor(out=sc[:, qs, 1, :], in0=sc[:, qs, 1, :], scalar=2.0, in1=pg[:, :, 0, :],
                                                       op0=ALU.mult, op1=ALU.add).then_inc(xtra_sb, 1)
                        nc.vector.tensor_scalar(sc[:, qs, 0, :], pg[:, :, 1, :], 4.0, None, ALU.mult)
                        v.wait_ge(xtra_sb, lv * (2 * NPG) + (2 * g + 1))
                        for h in range(2):
                            hs = slice(h * D, (h + 1) * D)
                            last = nc.vector.tensor_copy(bdb[hs, qs, hs], sc[hs, qs, 1, :])
                        last.then_inc(xtra_sb, 1)
                v.wait_ge(xtra_sb, 2 * NPG * EXTRA)
            nc.vector.scalar_tensor_tensor(out=em[:, :, :], in0=sc[:, :, 0, :], scalar=-0.5, in1=sc[:, :, 1, :],
                                           op0=ALU.mult, op1=ALU.add).then_inc(em_sb, 1)
            def f_low(k):
                v.wait_ge(f_hi, k + 1)
                nc.vector.tensor_tensor(fl[:, k * 8:(k + 1) * 8, :, :], f_twice(k), fh[:, k * 8:(k + 1) * 8, :, :].bitcast(F32),
                                        ALU.subtract).then_inc(f_lo, 1)

            for g in range(NG + 1):
                if g < NG and g % 2 == 0:
                    v.wait_ge(y_hi, g + 1)
                    nc.vector.tensor_tensor(ys[:, 0, 1, :], y[:, g, :], ys[:, 0, 0, :].bitcast(F32), ALU.subtract).then_inc(y_lo_dve, 1)
                if g == 0:
                    f_low(0)
                    f_low(1)
                if g < NG:
                    v.wait_ge(w_hi, g + 1)
                    nc.vector.tensor_tensor(wst[D:128, g % 2, :], py[g % 2][D:128, :], wst[D:128, g % 2, :].bitcast(F32),
                                            ALU.subtract).then_inc(w_lo, 1)
                if g in (1, 2):
                    f_low(g + 1)
                if g >= 1:
                    for c in range(2):
                        v.wait_ge(o_mm, 3 * (g - 1) + c + 1)
                        nc.vector.tensor_tensor(x[:, g - 1, c, :], pe_[c][0:KC, :], x[:, g - 1, c, :], ALU.add).then_inc(o_dve, 1)

        @block.tensor
        def _(pe):
            pe.wait_ge(p_in, 16)
            for c in range(NC):
                last = nc.tensor.matmul(pq[0][0:D, 0:D], pcs[:, c, :], pcs[:, c, :], start=(c == 0), stop=(c == NC - 1))
            last.then_inc(g_ps, 1)

            def y_part(g, r, c, k):
                if k == 0 and c == 0:
                    pe.wait_ge(x_lo_pool, g + 1)
                    if not isinstance(g, int) or g >= 2:
                        pe.wait_ge(y_sb, g - 1)
                if k == 0 and c == 2:
                    pe.wait_ge(x_lo_dve, g + 1)
                ins = nc.tensor.matmul(py[r][:, :], phl[:, c, :, :].rearrange("p k d -> p (k d)"), xs[:, r, c, k, :],
                                       start=(c == 0 and k == 0), stop=(c == NC - 1 and k == 1))
                if c == NC - 1 and k == 1:
                    ins.then_inc(y_mm, 1)

            def y_chunk(g, r, c):
                for k in range(2):
                    y_part(g, r, c, k)

            def block_fill(g, r):
                it = iter(range(NC))
                return lambda: y_chunk(g, r, next(it))

            def v_column(j):
                if j % (JH // 4) == 0:
                    pe.wait_ge(w_in[j // (JH // 4)], 16)
                for c in range(NC):
                    kc = KC + 1 if c == 0 else KC
                    last = nc.tensor.matmul(pe_[0][:, j * NB:(j + 1) * NB], wq[0:kc, c, j, :],
                                            silu[0:kc, c, :], start=(c == 0), stop=(c == NC - 1))
                if j == JH - 1:
                    last.then_inc(v_mm, 1)

            pe.wait_ge(masks, 7)
            newton_pe(pe, qr_mm, qr_sb, 1)
            pe.wait_ge(p_lo, 1)
            newton_pe(pe, qr_mm, qr_sb, 4, block_fill(0, 0))
            newton_pe(pe, qr_mm, qr_sb, 7, block_fill(1, 1))
            newton_pe(pe, qr_mm, qr_sb, 10, block_fill(2, 0))
            newton_pe(pe, qr_mm, qr_sb, 13, block_fill(3, 1))
            newton_pe(pe, qr_mm, qr_sb, 16, block_fill(4, 0))
            pe.wait_ge(pt_in, 16)
            k = 3 * NEWTON + 1
            pe.wait_ge(qr_sb, k)
            q1_pe(qr_mm)
            pe.wait_ge(silu_done, 1)
            pe.wait_ge(b_in, 16)
            columns = iter(range(JH))
            for j in range(SWEEPS):
                sweep_pe(pe, qr_mm, qr_sb, k + 1 + j)
                if j + NEWTON - 1 < NG:
                    for c in range(NC):
                        y_chunk(j + NEWTON - 1, (j + NEWTON - 1) % 2, c)
                for _ in range(JH * (j + 1) // SWEEPS - JH * j // SWEEPS):
                    v_column(next(columns))
            k += SWEEPS + 1
            sweep_pe(pe, qr_mm, qr_sb, k)
            pe.wait_ge(st_sb, 1)
            for j in range(3):
                last = nc.tensor.matmul(pq[1][0:1, j * D:(j + 1) * D], stats[:, j:j + 1], ident[0:D, 0:D], start=True, stop=True)
            last.then_inc(st_mm, 1)
            pe.wait_ge(flags, 1)
            redo = pe.value_load(redo_qr[0:1, 0:1], min_val=0, max_val=1)
            with pe.If(redo):
                general_pe(pe)
            pe.wait_ge(final, 1)
            nc.tensor.matmul(pq[1][:, 0:N], xd[:, :, :].rearrange("p k d -> p (k d)"), pts[:, :],
                             start=True, stop=True).then_inc(uu_mm, 1)

            pe.wait_ge(vss_sb, 1)
            nc.tensor.matmul(pe_[1][:, 0:NB], onesm[:, :], vss[:, :], start=True, stop=True).then_inc(vss_mm, 1)

            def products(g, left, right, done):
                for q in range(PG):
                    p = g * PG + q
                    last = nc.tensor.matmul(pe_[g][:, q * 2 * D:(q + 1) * 2 * D], left[:, p, :],
                                            right[:, p, :, :].rearrange("p k d -> p (k d)"), start=True, stop=True)
                last.then_inc(done, 1)

            pe.wait_ge(bd0, 1)
            for g in range(NPG):
                for q in range(PG):
                    last = nc.tensor.matmul(pe_[g][:, q * D:(q + 1) * D], bdb[:, g * PG + q, :], zb[:, g * PG + q, 1, :],
                                            start=True, stop=True)
                last.then_inc(ex_mm, 1)
            for g in range(NPG):
                pe.wait_ge(ex_dve, g + 1)
                products(g, bdz, zb, ex_mm)
            for k, right in ((1, r1), (2, zb)):
                for g in range(NPG):
                    pe.wait_ge(ex_dve, k * NPG + g + 1)
                    products(g, bdz2, right, ex_mm)
            with pe.Fori(0, LEVELS) as lv:
                for g in range(NPG):
                    pe.wait_ge(ex_act, lv * NPG + (2 * NPG + g + 1))
                    pe.wait_ge(ex_pool, lv * NPG + (g + 1))
                    products(g, bdb, sc, ex_mm)
            pe.wait_ge(ex_pool, NPG * (1 + LEVELS))
            pe.wait_ge(ex_act, (3 + LEVELS) * NPG)
            pe.wait_ge(flags, 2)
            deeper = pe.value_load(more[0:1, 0:1], min_val=0, max_val=1)
            with pe.If(deeper):
                for g in range(NPG):
                    products(g, bdb, sc, xtra_mm)
                with pe.Fori(1, EXTRA) as lv:
                    for g in range(NPG):
                        pe.wait_ge(xtra_sb, lv * (2 * NPG) + (2 * g + 2 - 2 * NPG))
                        products(g, bdb, sc, xtra_mm)
            def f_products(k):
                h, q0 = k // 2, k % 2 * 8
                if k >= 2:
                    pe.wait_ge(f_lo, k - 1)
                nc.tensor.matmul(pq[k % 2][:, :], bdx[h * D:(h + 1) * D, :],
                                 em[h * D:(h + 1) * D, q0:q0 + 8, :].rearrange("p q d -> p (q d)"), start=True, stop=True).then_inc(f_mm, 1)

            pe.wait_ge(final, 8)
            pe.wait_ge(em_sb, 1)
            f_products(0)
            pe.wait_ge(uu_sb, 2)
            f_products(1)

            for g in range(NG + 1):
                if g < NG:
                    pe.wait_ge(y_lo_dve, g // 2 + 1)
                    if g % 2:
                        pe.wait_ge(y_lo_pool, g // 2 + 1)
                    if g >= 2:
                        pe.wait_ge(w_lo, g - 1)
                    if g % 4 == 0:
                        pe.wait_ge(f_lo, g // 4 + 1)
                    for r in range(GB):
                        b = g * GB + r
                        for k in range(2):
                            for f in (fh, fl):
                                last = nc.tensor.matmul(py[g % 2][:, r * T:(r + 1) * T],
                                                        f[:, b, :, :].rearrange("p k d -> p (k d)"),
                                                        ys[:, g % 2, k, r * T:(r + 1) * T],
                                                        start=(k == 0 and f is fh), stop=(k == 1 and f is fl))
                    last.then_inc(w_mm, 1)
                if g in (0, 1):
                    f_products(g + 2)
                if g >= 1:
                    k = g - 1
                    pe.wait_ge(w_lo, k + 1)
                    for c in range(NC):
                        bank = pe_[c] if c < 2 else pe_[2 + k % 2]
                        if c < 2 and k >= 1:
                            pe.wait_ge(o_dve, 2 * (k - 1) + c + 1)
                        if c == 2 and k >= 2:
                            pe.wait_ge(o_act, k - 1)
                        for j, uu in enumerate((uuh, uul)):
                            last = nc.tensor.matmul(bank[0:KC, :], uu[:, c * KC:(c + 1) * KC], wst[:, k % 2, :],
                                                    start=(j == 0), stop=(j == 1))
                        last.then_inc(o_mm, 1)


def kernel(x, cond_1152, L0_cond_P, L0_cond_W, L0_cond_b):
    import numpy as np
    import concourse.bacc as bacc
    from concourse.bass_utils import run_bass_kernel_spmd

    xb = np.ascontiguousarray(np.asarray(x).reshape(NG, BT, NC, KC).transpose(0, 3, 2, 1))
    cond = np.ascontiguousarray(np.asarray(cond_1152).reshape(NB, NC, KC).transpose(2, 1, 0))
    P = np.asarray(L0_cond_P)
    pc = np.ascontiguousarray(P.reshape(NC, KC, D).transpose(1, 0, 2))
    pt = np.ascontiguousarray(P.T)
    iu, ju = np.triu_indices(D, k=1)
    where = np.zeros((D, D), np.int64)
    where[iu, ju] = where[ju, iu] = np.arange(len(iu))
    low = np.tri(Q, dtype=bool)
    folded = np.where(low, where[Q:, Q:], where[:Q, :Q])
    where = np.stack([folded, where[:Q, Q:]]).reshape(2, Q, 2, JH).transpose(3, 2, 0, 1).reshape(JH, 4 * Q)
    W = np.asarray(L0_cond_W)
    wd = np.ascontiguousarray(W[where].reshape(JH, 4 * Q, NC, KC).transpose(3, 2, 0, 1))
    bd = np.ascontiguousarray(np.asarray(L0_cond_b)[where][None])

    nc = bacc.Bacc("TRN2", target_bir_lowering=False, num_devices=1)
    arrays = {"xb": xb, "cond": cond, "pc": pc, "pt": pt, "wd": wd, "bd": bd}
    args = [nc.dram_tensor(k, a.shape, mybir.dt.from_np(a.dtype), kind="ExternalInput").ap() for k, a in arrays.items()]
    out = nc.dram_tensor("out", xb.shape, F32, kind="ExternalOutput").ap()
    rotation_kernel(nc, *args, out)
    r = run_bass_kernel_spmd(nc, [arrays], core_ids=[0])
    got = r.results[0]["out"]
    return np.ascontiguousarray(got.transpose(0, 3, 2, 1)).reshape(NB, T, N)
```

```python
from contextlib import ExitStack

import concourse.bass as bass
from concourse import mybir

F32 = mybir.dt.float32
F32R = mybir.dt.float32r
BF16 = mybir.dt.bfloat16
I32 = mybir.dt.int32
ALU = mybir.AluOpType
ACT = mybir.ActivationFunctionType
AX = mybir.AxisListType

NB = 32
T = 256
N = 288
D = 64
NC = 3
KC = N // NC
GB = 2
NG = NB // GB
BT = GB * T
NQ = NB // 2
PG = 4
NPG = NQ // PG
Q = 32
JH = Q // 2
BANK = 512
NV = 4

IDLE_START, IDLE_G, IDLE_N0, IDLE_N, IDLE_S2, IDLE_S3, IDLE_F, IDLE_B, IDLE_1, IDLE_2, IDLE_3, IDLE_4, IDLE_E = 6, 2, 3, 0, 2, 6, 3, 2, 4, 4, 4, 4, 6
LEVELS = 3
EXTRA = 10
NORM_LIMIT = 21.0
NEWTON = 6
SWEEPS = 12
GENERAL_NEWTON = 24
NEWTON_TOL = 1e-4
SIGN_MARGIN = 256.0

C2, C3, C4, C5, C6 = 0.0416666571657677, 0.00138887393400706, 2.479333172713527e-05, 2.734932968796656e-07, 1.8413557053625046e-09
S1, S2, S3, S4, S5 = 0.166666591359001, 0.008333188068671657, 0.00019832099913381806, 2.7302947877662567e-06, 2.1809401449776777e-08


def rotation_kernel(nc, xb, cond, pc, pt, wd, bd, out):
    with ExitStack() as ctx:
        def sb(name, shape, dt=F32):
            return ctx.enter_context(nc.sbuf_tensor(name, shape, dt))

        def sem(name):
            return ctx.enter_context(nc.semaphore(name))

        x = sb("x", [KC, NG, NC, BT])
        def at_room(*tensors):
            with ExitStack() as room:
                return [room.enter_context(nc.sbuf_tensor(name, shape, dt)) for name, shape, dt in tensors]

        wq, xs = at_room(("wq", [KC + 1, NC, NV, BANK], F32), ("xs", [KC, 2, NC, 2, BT], F32R))
        pair = [128, NQ, 2, D]
        bdz, zb, zz, r1, sc, bdz2 = at_room(
            ("bdz", [128, NQ, 128], F32), ("zb", pair, F32), ("zz", pair, F32),
            ("r1", pair, F32), ("sc", pair, F32), ("bdz2", [128, NQ, 128], F32))
        mid = bdz[:, :, :].rearrange("p q (k d) -> p q k d", k=2)
        flat = zz[:, :, :, :].rearrange("p q k d -> p (q k d)")
        v1, v2, tri1, tri2 = (flat[:, k:k + 512].rearrange("p (q j) -> p q j", q=NQ) for k in range(0, 2048, 512))
        fh, em, tmp, fl, ys = at_room(
            ("fh", [128, NB, 2, D], F32R), ("em", [128, NQ, D], F32), ("tmp", [KC, 2, BT], F32),
            ("fl", [128, NB, 2, D], F32R), ("ys", [128, 2, 2, BT], F32R))
        room = sb("room", [128, 12288])
        y = sb("y", [128, NG, BT])
        pcs = sb("pcs", [KC, NC, D])
        phl = sb("phl", [KC, NC, 2, D], F32R)
        pts = sb("pts", [D, N])
        cnd = sb("cnd", [KC, NC, NB])
        cexp = sb("cexp", [KC, NC, NB])
        silu = sb("silu", [KC + 1, NC, NB])
        ident = sb("ident", [128, 128])
        neg3 = sb("neg3", [D, D])
        pos2 = sb("pos2", [D, D])
        phi = sb("phi", [D, D])
        su = sb("su", [D, D])
        suh = sb("suh", [D, D])
        colm = sb("colm", [D, 2 * D])
        onesm = sb("onesm", [128, 128])
        upm = sb("upm", [128, Q])
        lom = sb("lom", [128, Q])
        idle = sb("idle", [128, BT], BF16)
        gs = sb("gs", [D, 2 * D])
        xx = sb("xx", [D, 2 * D])
        tm = sb("tm", [D, D])
        mm = sb("mm", [D, 2 * D])
        junk = sb("junk", [D, 2 * D])
        small = sb("small", [D, 8])
        qq = sb("qq", [D, 2 * D])
        qh = sb("qh", [D, 1])
        cc = sb("cc", [D, 2 * D])
        cl = sb("cl", [D, 2 * D])
        ul = sb("ul", [D, 2 * D])
        ul2 = sb("ul2", [D, 2 * D])
        hp = sb("hp", [D, 1])
        uh = sb("uh", [D, 1])
        ur = sb("ur", [D, 1])
        stats = sb("stats", [D, 4])
        st1 = sb("st1", [1, 8])
        redo_qr = sb("redo_qr", [1, 1], I32)
        phij = sb("phij", [D, D])
        inact = sb("inact", [D, D])
        sg = sb("sg", [128, 1])
        xd = sb("xd", [D, 2, D])
        bdx = sb("bdx", [128, 128])
        uuh = sb("uuh", [128, N], F32R)
        uul = sb("uul", [128, N], F32R)
        vsq = sb("vsq", [128, BANK])
        vss = sb("vss", [128, NB])
        cnt = sb("cnt", [128, 1])
        nfac2 = sb("nfac2", [128, 1])
        fac = sb("fac", [128, 1])
        more = sb("more", [1, 1], I32)
        (vt,) = at_room(("vt", [Q, 2, NB, Q], F32))
        bdb = sb("bdb", [128, NQ, 128])
        (vtri,) = at_room(("vtri", [128, 1024], F32))
        tri3, tri4 = (vtri[:, k * 512:(k + 1) * 512].rearrange("p (q j) -> p q j", q=NQ) for k in range(2))
        wst = sb("wst", [128, 2, BT], F32R)

        ps = [ctx.enter_context(nc.psum_tensor(f"ps{i}", [128, 512], F32)) for i in range(8)]
        pq = ps[0:2]
        py = ps[2:4]
        pe_ = ps[4:8]
        out_banks = (pe_[0], pq[0], pq[1]), (pe_[1], pe_[2], pe_[3])

        p_in, pt_in, c_in = sem("p_in"), sem("pt_in"), sem("c_in")
        w_in = [sem(f"w_in{i}") for i in range(4)]
        b_in = sem("b_in")
        x_in = [sem("x_in0"), sem("x_in1")]
        masks = sem("masks")
        idle_ones = sem("idle_ones")
        pool_chain = sem("pool_chain")
        ones_row = sem("ones_row")
        exp_done, silu_done = sem("exp_done"), sem("silu_done")
        dv = sem("dv")
        g_ps, gdiag, groot = sem("g_ps"), sem("gdiag"), sem("groot")
        qr_mm, qr_sb = sem("qr_mm"), sem("qr_sb")
        xs_used, y_sb = sem("xs_used"), sem("y_sb")
        v_mm, b_sb = sem("v_mm"), sem("b_sb")
        vt_sb, vsq_done, vss_mm, v1_sb, v2_sb = sem("vt_sb"), sem("vsq_done"), sem("vss_mm"), sem("v1_sb"), sem("v2_sb")
        tri_pool = sem("tri_pool")
        fac_sb, b_scaled = sem("fac_sb"), sem("b_scaled")
        p_hi, p_lo, x_hi, x_lo_pool, x_lo_dve = sem("p_hi"), sem("p_lo"), sem("x_hi"), sem("x_lo_pool"), sem("x_lo_dve")
        bd0, bdz_clear, bdb_clear = sem("bd0"), sem("bdz_clear"), sem("bdb_clear")
        low_act, low_sb = sem("low_act"), sem("low_sb")
        flags, more_sb = sem("flags"), sem("more_sb")
        st_mm, st_sb = sem("st_mm"), sem("st_sb")
        ex_mm = sem("ex_mm")
        ex_act, ex_dve, ex_pool = sem("ex_act"), sem("ex_dve"), sem("ex_pool")
        gen_mm, gen_sb, gen_dv = sem("gen_mm"), sem("gen_sb"), sem("gen_dv")
        xtra_mm, xtra_sb = sem("xtra_mm"), sem("xtra_sb")
        final = sem("final")
        uu_mm, uu_sb = sem("uu_mm"), sem("uu_sb")
        em_sb, f_mm, f_hi, f_lo = sem("em_sb"), sem("f_mm"), sem("f_hi"), sem("f_lo")
        y_hi, y_lo_dve, y_lo_pool = sem("y_hi"), sem("y_lo_dve"), sem("y_lo_pool")
        w_mm, w_hi, w_lo = sem("w_mm"), sem("w_hi"), sem("w_lo")
        o_mm, o_dve, o_act, o_pool = sem("o_mm"), sem("o_dve"), sem("o_act"), sem("o_pool")
        stored = sem("stored")

        block = ctx.enter_context(nc.Block())

        @block.sync
        def _(sp):
            sp.dma_start(pcs[:, :, :], pc).then_inc(p_in, 16)
            sp.dma_start(pts[:, :], pt).then_inc(pt_in, 16)
            sp.dma_start(cnd[:, :, :], cond).then_inc(c_in, 16)
            sp.dma_start(x[:, 0, :, :], xb[0, :, :, :]).then_inc(x_in[0], 16)
            sp.dma_start(x[:, 1, :, :], xb[1, :, :, :]).then_inc(x_in[1], 16)
            sp.dma_start(wq[KC:KC + 1, 0, :, :], bd).then_inc(b_in, 16)

            for k in range(4):
                for r in range(2):
                    g = 2 + 2 * k + r
                    sp.wait_ge(x_in[r], 16 * (k + 1))
                    sp.dma_start(x[:, g, :, :], xb[g, :, :, :]).then_inc(x_in[r], 16)
                sp.dma_start(wq[0:KC, :, k, :], wd[:, :, k, :]).then_inc(w_in[k], 16)
            for k in range(4, NG // 2 - 1):
                for r in range(2):
                    g = 2 + 2 * k + r
                    sp.wait_ge(x_in[r], 16 * (k + 1))
                    sp.dma_start(x[:, g, :, :], xb[g, :, :, :]).then_inc(x_in[r], 16)

            for g in range(NG):
                sp.wait_ge(o_dve, 2 * g + 2)
                sp.wait_ge(o_pool, g + 1)
                sp.dma_start(out[g, :, :, :], x[:, g, :, :]).then_inc(stored, 16)
            sp.wait_ge(stored, 16 * NG)

        @block.gpsimd
        def _(pool):
            n = [0]

            def link(ins):
                n[0] += 1
                ins.then_inc(pool_chain, 1)
                pool.wait_ge(pool_chain, n[0])

            link(nc.gpsimd.memset(mm[:, D:2 * D], 0.0))
            nc.gpsimd.memset(idle[:, :], 1.0).then_inc(idle_ones, 1)
            link(nc.gpsimd.memset(ident[:, :], 0.0))
            nc.gpsimd.affine_select(out=ident[:, :], in_=ident[:, :], compare_op=ALU.not_equal, fill=1.0,
                                    base=0, pattern=[[-1, 128]], channel_multiplier=1).then_inc(masks, 1)
            def diagonal(dst, val):
                link(nc.gpsimd.memset(dst[:, :], 0.0))
                nc.gpsimd.affine_select(out=dst[:, :], in_=dst[:, :], compare_op=ALU.not_equal, fill=val,
                                        base=0, pattern=[[-1, D]], channel_multiplier=1).then_inc(masks, 1)

            def upper(dst, val):
                link(nc.gpsimd.memset(dst[:, :], val))
                return nc.gpsimd.affine_select(out=dst[:, :], in_=dst[:, :], compare_op=ALU.is_gt, fill=0.0,
                                               base=0, pattern=[[1, D]], channel_multiplier=-1)

            diagonal(neg3, -3.0)
            link(upper(phi, -1.0))
            nc.gpsimd.affine_select(out=phi[:, :], in_=phi[:, :], compare_op=ALU.not_equal, fill=-0.5,
                                    base=0, pattern=[[-1, D]], channel_multiplier=1).then_inc(masks, 1)
            nc.gpsimd.memset(silu[KC:KC + 1, :, :], 1.0).then_inc(masks, 1)
            diagonal(pos2, 2.0)
            upper(su, 1.0).then_inc(masks, 1)
            upper(suh, 0.5).then_inc(masks, 1)
            for dst, sign in ((upm, 1), (lom, -1)):
                link(nc.gpsimd.memset(dst[:, :], 2.0 ** -LEVELS))
                for k in range(4):
                    rows = dst[k * Q:(k + 1) * Q, :]
                    link(nc.gpsimd.affine_select(out=rows, in_=rows, compare_op=ALU.is_gt, fill=0.0,
                                                 base=0, pattern=[[sign, Q]], channel_multiplier=-sign))
            link(nc.gpsimd.memset(colm[:, 0:D], 1.0))
            link(nc.gpsimd.memset(colm[:, D:2 * D], 0.0))
            link(nc.gpsimd.memset(onesm[:, :], 1.0))

            with pool.Fori(0, NG // 2) as h:
                for r in range(2):
                    for c in range(2):
                        pool.wait_ge(x_hi, h * 6 + (3 * r + c + 1))
                        nc.gpsimd.tensor_tensor(xs[:, r, c, 1, :], x[:, bass.ds(h * 2 + r, 1), c, :].rearrange("p a t -> p (a t)"),
                                                xs[:, r, c, 0, :].bitcast(F32), ALU.subtract).then_inc(x_lo_pool, 1)
            pool.wait_ge(v1_sb, 4)
            nc.gpsimd.memset(bdb[:, :, :], 0.0).then_inc(bdb_clear, 1)
            pool.wait_ge(v2_sb, 1)
            for dst, src, mask in ((tri3, v2, upm), (tri4, v1, lom)):
                nc.gpsimd.tensor_tensor(dst, src, mask[:, :].rearrange("p (a j) -> p a j", a=1).to_broadcast([128, NQ, Q]),
                                        ALU.mult).then_inc(tri_pool, 1)
            v1_flat = v1[:, :, :].rearrange("p q j -> p (q j)")
            nc.gpsimd.tensor_tensor(vsq[:, :], v1_flat, v1_flat, ALU.mult).then_inc(vsq_done, 1)
            nc.gpsimd.memset(bdz[:, :, :], 0.0).then_inc(bdz_clear, 1)
            pool.wait_ge(xs_used, 3 * NG)
            nc.gpsimd.memset(bdz2[:, :, :], 0.0).then_inc(bdz_clear, 1)

            for k, op in ((0, ALU.subtract), (1, ALU.add)):
                pool.wait_ge(low_act, k + 1)
                nc.gpsimd.tensor_tensor(sc[:, :, k, :], sc[:, :, k, :], zb[:, :, k, :], op).then_inc(low_sb, 1)

            with pool.Fori(0, LEVELS + 1) as lv:
                for g in range(NPG):
                    qs = slice(g * PG, (g + 1) * PG)
                    pool.wait_ge(ex_dve, lv * NPG + (3 * NPG + g + 1))
                    nc.gpsimd.tensor_tensor(bdb[0:D, qs, 0:D], sc[0:D, qs, 1, :],
                                            onesm[0:D, 0:D].rearrange("p (a d) -> p a d", a=1).to_broadcast([D, PG, D]),
                                            ALU.mult).then_inc(ex_pool, 1)

            def y_low_odd(g):
                pool.wait_ge(y_hi, g + 1)
                nc.gpsimd.tensor_tensor(ys[:, 1, 1, :], y[:, g, :], ys[:, 1, 0, :].bitcast(F32), ALU.subtract).then_inc(y_lo_pool, 1)

            y_low_odd(1)
            for k in range(NG):
                if k % 2 == 0 and k + 3 < NG:
                    y_low_odd(k + 3)
                pool.wait_ge(o_act, k + 1)
                nc.gpsimd.tensor_tensor(x[:, k, 2, :], x[:, k, 2, :], tmp[:, k % 2, :], ALU.add).then_inc(o_pool, 1)

        def f_twice(k):
            return pe_[k][:, :].rearrange("p (b a d) -> p b a d", b=8, a=1).to_broadcast([128, 8, 2, D])

        @block.scalar
        def _(act):
            act.wait_ge(c_in, 16)
            nc.scalar.activation(cexp[:, :, :], cnd[:, :, :], ACT.Exp, scale=-1.0).then_inc(exp_done, 1)
            act.wait_ge(gdiag, 1)
            nc.scalar.activation(small[:, 1:2], small[:, 0:1], ACT.Sqrt).then_inc(groot, 1)

            act.wait_ge(p_in, 16)
            nc.scalar.activation(phl[:, :, 0, :], pcs[:, :, :], ACT.Copy).then_inc(p_hi, 1)
            for r in range(2):
                act.wait_ge(x_in[r], 16)
                for c in range(NC):
                    nc.scalar.activation(xs[:, r, c, 0, :], x[:, r, c, :], ACT.Copy).then_inc(x_hi, 1)

            def y_pair(h):
                for r in range(2):
                    act.wait_ge(x_in[r], h * 16 + 32)
                    for c in range(NC):
                        act.wait_ge(xs_used, h * 6 + (3 * r + c + 1))
                        nc.scalar.activation(xs[:, r, c, 0, :], x[:, bass.ds(h * 2 + (2 + r), 1), c, :].rearrange("p a t -> p (a t)"),
                                             ACT.Copy).then_inc(x_hi, 1)
                    nc.scalar.activation(y[:, bass.ds(h * 2 + r, 1), :].rearrange("p a t -> p (a t)"),
                                         py[r][:, :], ACT.Copy).then_inc(y_sb, 1)

            def quadrants(r):
                act.wait_ge(vt_sb, 2 * r + 2)
                act.wait_ge(v_mm, NV)
                for h in range(2):
                    k = (2 * h + r) * Q
                    nc.scalar.activation(v1[k:k + Q, :, :], vt[:, r, h * NQ:(h + 1) * NQ, :], ACT.Copy).then_inc(v1_sb, 1)

            with act.Fori(0, 6) as h:
                y_pair(h)
            quadrants(0)
            quadrants(1)
            with act.Fori(6, NG // 2 - 1) as h:
                y_pair(h)
            for g in (NG - 2, NG - 1):
                act.wait_ge(xs_used, 3 * g + 3)
                nc.scalar.activation(y[:, g, :], py[g % 2][:, :], ACT.Copy).then_inc(y_sb, 1)

            for h in range(2):
                nc.scalar.activation(zb[h * D:h * D + Q, :, 1, Q:D], v1[h * D + Q:(h + 1) * D, :, :], ACT.Copy,
                                     scale=2.0 ** -LEVELS).then_inc(b_sb, 1)
            act.wait_ge(v2_sb, 1)
            for h in range(2):
                nc.scalar.activation(zb[h * D + Q:(h + 1) * D, :, 1, 0:Q], v2[h * D + Q:(h + 1) * D, :, :], ACT.Copy,
                                     scale=-2.0 ** -LEVELS).then_inc(b_sb, 1)

            act.wait_ge(b_sb, 8)
            act.wait_ge(bdb_clear, 1)
            nc.scalar.activation(bdb[D:128, :, D:128], zb[D:128, :, 1, :], ACT.Copy).then_inc(bd0, 1)

            act.wait_ge(fac_sb, 1)
            for g in range(NPG):
                qs = slice(g * PG, (g + 1) * PG)
                act.wait_ge(ex_mm, g + 1)
                nc.scalar.activation(zb[:, qs, 0, :], pe_[g][:, 0:PG * D].rearrange("p (q d) -> p q d", q=PG),
                                     ACT.Copy, scale=nfac2[:, 0:1]).then_inc(ex_act, 1)
                nc.scalar.activation(zb[:, qs, 1, :], zb[:, qs, 1, :], ACT.Copy, scale=fac[:, 0:1]).then_inc(b_scaled, 1)
            for g in range(NPG):
                act.wait_ge(ex_mm, NPG + g + 1)
                nc.scalar.activation(zz[:, g * PG:(g + 1) * PG, :, :].rearrange("p q k d -> p (q k d)"), pe_[g][:, :],
                                     ACT.Copy).then_inc(ex_act, 1)
            act.wait_ge(ex_act, 2 * NPG)
            for k, factor in ((0, -2 * C2), (1, S1)):
                nc.scalar.activation(sc[:, :, k, :], zz[:, :, k, :], ACT.Copy, scale=factor).then_inc(low_act, 1)
            for g in range(NPG):
                qs = slice(g * PG, (g + 1) * PG)
                act.wait_ge(ex_dve, 3 * NPG + g + 1)
                nc.scalar.activation(bdb[D:128, qs, D:128], sc[D:128, qs, 1, :], ACT.Copy).then_inc(ex_act, 1)
            with act.Fori(0, LEVELS) as lv:
                for g in range(NPG):
                    qs = slice(g * PG, (g + 1) * PG)
                    pg = pe_[g][:, :].rearrange("p (q k d) -> p q k d", q=PG, k=2)
                    act.wait_ge(ex_dve, lv * NPG + (4 * NPG + g + 1))
                    nc.scalar.activation(bdb[D:128, qs, D:128], sc[D:128, qs, 1, :], ACT.Copy)
                    nc.scalar.activation(sc[:, qs, 0, :], pg[:, :, 1, :], ACT.Copy, scale=4.0).then_inc(ex_act, 1)

            def y_high(g):
                if g >= 2:
                    act.wait_ge(w_mm, g - 1)
                nc.scalar.activation(ys[:, g % 2, 0, :], y[:, g, :], ACT.Copy).then_inc(y_hi, 1)

            act.wait_ge(em_sb, 2)
            y_high(0)
            def f_high(k):
                act.wait_ge(f_mm, k + 1)
                nc.scalar.activation(fh[:, k * 8:(k + 1) * 8, :, :], f_twice(k), ACT.Copy).then_inc(f_hi, 1)

            y_high(1)
            f_high(0)
            for g in range(NG + 1):
                if g < NG:
                    act.wait_ge(w_mm, g + 1)
                    if g >= 2:
                        act.wait_ge(o_mm, 3 * (g - 1))
                    nc.scalar.activation(wst[:, g % 2, :], py[g % 2][:, :], ACT.Copy).then_inc(w_hi, 1)
                if g + 2 < NG:
                    y_high(g + 2)
                if g == 0:
                    f_high(1)
                if g == 1:
                    f_high(2)
                    f_high(3)
                if g >= 1:
                    k = g - 1
                    act.wait_ge(o_mm, 3 * k + 3)
                    if k >= 2:
                        act.wait_ge(o_pool, k - 1)
                    nc.scalar.activation(tmp[:, k % 2, :], out_banks[k % 2][2][0:KC, :], ACT.Copy).then_inc(o_act, 1)

        def newton_dve(v, mmsem, sbsem, k, active=None, check=False):
            v.wait_ge(mmsem, k + 1)
            nc.vector.tensor_copy(tm[:, :], pq[0][0:D, 0:D]).then_inc(sbsem, 1)
            v.wait_ge(mmsem, k + 2)
            if active is None:
                nc.vector.tensor_tensor(mm[:, 0:D], pq[1][0:D, 0:D], phi[:, :], ALU.mult).then_inc(sbsem, 1)
            else:
                v.wait_ge(gen_dv, active - 1)
                nc.vector.tensor_tensor(junk[:, 0:D], pq[1][0:D, 0:D], phij[:, :], ALU.mult).then_inc(gen_dv, 1)
                v.wait_ge(gen_dv, active)
                nc.vector.tensor_tensor(mm[:, 0:D], junk[:, 0:D], inact[:, :], ALU.add).then_inc(sbsem, 1)
            if check:
                nc.vector.tensor_tensor(junk[:, 0:D], pq[1][0:D, 0:D], pos2[:, :], ALU.add).then_inc(gdiag, 1)
            v.wait_ge(mmsem, k + 3)
            nc.vector.tensor_copy(xx[:, :], pq[0][0:D, 0:2 * D]).then_inc(sbsem, 1)

        def newton_pe(pe, mmsem, sbsem, k, filler=None):
            f = filler or (lambda: None)
            pe.wait_ge(sbsem, k)
            nc.tensor.matmul(pq[0][:, 0:D], gs[:, :], xx[:, 0:D], start=True, stop=True).then_inc(mmsem, 1)
            nc.tensor.matmul(pq[1][:, 0:D], ident[0:D, :], neg3[:, :], start=True, stop=False)
            f()
            pe.wait_ge(sbsem, k + 1)
            nc.tensor.matmul(pq[1][:, 0:D], xx[:, :], tm[:, :], start=False, stop=True).then_inc(mmsem, 1)
            f()
            pe.wait_ge(sbsem, k + 2)
            nc.tensor.matmul(pq[0][:, D:2 * D], mm[:, :], xx[:, D:2 * D], start=True, stop=True)
            nc.tensor.matmul(pq[0][0:D, 0:D], xx[:, D:2 * D], mm[:, 0:D], start=True, stop=True).then_inc(mmsem, 1)
            f()

        def q1_pe(mmsem):
            nc.tensor.matmul(pq[1][0:D, 0:D], pts[:, 0:D], xx[:, 0:D], start=True, stop=True)
            nc.tensor.matmul(pq[1][0:D, D:2 * D], xx[:, 0:D], pts[:, 0:D], start=True, stop=True).then_inc(mmsem, 1)

        def q1_dve(v, mmsem, k, sbsem, dvsem, base):
            v.wait_ge(mmsem, k)
            nc.vector.tensor_copy(qq[:, :], pq[1][0:D, 0:2 * D]).then_inc(dvsem, 1)
            v.wait_ge(dvsem, base + 1)
            nc.vector.tensor_tensor_reduce(out=junk[:, 0:D], in0=qq[:, 0:D], in1=ident[0:D, 0:D], scale=0.5, scalar=-0.5,
                                           op0=ALU.mult, op1=ALU.add, accum_out=qh[:, 0:1]).then_inc(dvsem, 1)
            v.wait_ge(dvsem, base + 2)
            nc.vector.memset(ul[:, :], 0.0).then_inc(sbsem, 1)

        def sweep_pe(pe, mmsem, sbsem, k):
            pe.wait_ge(sbsem, k)
            nc.tensor.matmul(pq[0][:, D:2 * D], ul[:, :], ul[:, D:2 * D], start=True, stop=True)
            nc.tensor.matmul(pq[0][0:D, 0:D], ul[:, D:2 * D], ul[:, 0:D], start=True, stop=True).then_inc(mmsem, 1)

        def x_low(v, g, r):
            v.wait_ge(x_hi, g * 3 + 3)
            src = x[:, g, 2, :] if isinstance(g, int) else x[:, bass.ds(g, 1), 2, :].rearrange("p a t -> p (a t)")
            nc.vector.tensor_tensor(xs[:, r, 2, 1, :], src, xs[:, r, 2, 0, :].bitcast(F32), ALU.subtract).then_inc(x_lo_dve, 1)

        SWEEP_DV = 5

        def sweep_dve(v, mmsem, k, sbsem, dvsem, base, dst):
            v.wait_ge(mmsem, k)
            nc.vector.tensor_tensor_reduce(out=junk[:, 0:D], in0=pq[0][0:D, 0:D], in1=ident[0:D, 0:D],
                                           scale=-0.5, scalar=qh[:, 0:1], op0=ALU.mult, op1=ALU.add,
                                           accum_out=hp[:, 0:1]).then_inc(dvsem, 1)
            nc.vector.tensor_tensor(cc[:, :], qq[:, :], pq[0][0:D, 0:2 * D], ALU.subtract).then_inc(dvsem, 1)
            v.wait_ge(dvsem, base + 1)
            nc.vector.scalar_tensor_tensor(out=uh[:, :], in0=hp[:, :], scalar=-0.5, in1=hp[:, :],
                                           op0=ALU.is_ge, op1=ALU.add).then_inc(dvsem, 1)
            v.wait_ge(dvsem, base + 2)
            nc.vector.tensor_scalar(cl[:, :], cc[:, :], 4.0, -4.0, ALU.min, ALU.max).then_inc(dvsem, 1)
            v.wait_ge(dvsem, base + 3)
            nc.vector.reciprocal(ur[:, :], uh[:, :]).then_inc(dvsem, 1)
            v.wait_ge(dvsem, base + 4)
            nc.vector.tensor_tensor(dst[:, 0:D], cl[:, 0:D], su[:, :], ALU.mult)
            v.wait_ge(dvsem, base + 5)
            nc.vector.scalar_tensor_tensor(out=dst[:, D:2 * D], in0=cl[:, D:2 * D], scalar=ur[:, 0:1],
                                           in1=suh[:, :], op0=ALU.mult, op1=ALU.mult).then_inc(sbsem, 1)

        GEN_STEPS = D * GENERAL_NEWTON
        GEN_X = 3 * GEN_STEPS + 1

        def general_dve(v):
            for h in range(2):
                last = nc.vector.tensor_scalar(xx[:, h * D:(h + 1) * D], ident[0:D, 0:D], small[:, 2:3], None, ALU.mult)
            last.then_inc(gen_sb, 1)
            with v.Fori(0, D) as j:
                per = GENERAL_NEWTON + 3
                upto = colm[:, bass.ds(D - 1 - j, D)]
                nc.vector.tensor_tensor(phij[:, :], phi[:, :], upto, ALU.mult).then_inc(gen_dv, 1)
                nc.vector.tensor_tensor(junk[:, 0:D], ident[0:D, 0:D], upto, ALU.mult).then_inc(gen_dv, 1)
                v.wait_ge(gen_dv, j * per + 2)
                nc.vector.tensor_tensor(inact[:, :], ident[0:D, 0:D], junk[:, 0:D], ALU.subtract).then_inc(gen_dv, 1)
                with v.Fori(0, GENERAL_NEWTON) as i:
                    newton_dve(v, gen_mm, gen_sb, j * (3 * GENERAL_NEWTON) + i * 3, active=j * per + (i + 4))
            base = D * (GENERAL_NEWTON + 3)
            q1_dve(v, gen_mm, GEN_X, gen_sb, gen_dv, base)
            with v.Fori(0, D) as i:
                sweep_dve(v, gen_mm, i + (GEN_X + 1), gen_sb, gen_dv, i * SWEEP_DV + (base + 2), ul)

        def general_pe(pe):
            with pe.Fori(0, GEN_STEPS) as n:
                newton_pe(pe, gen_mm, gen_sb, n * 3 + 1)
            pe.wait_ge(gen_sb, GEN_X)
            q1_pe(gen_mm)
            with pe.Fori(0, D) as i:
                sweep_pe(pe, gen_mm, gen_sb, i + (GEN_X + 1))

        @block.vector
        def _(v):
            count = [0]

            def out_(ins):
                ins.then_inc(dv, 1)
                count[0] += 1
                return count[0]

            def start_x():
                for h in range(2):
                    last = nc.vector.tensor_scalar(xx[:, h * D:(h + 1) * D], ident[0:D, 0:D], small[:, 2:3], None, ALU.mult)
                return last

            v.wait_ge(masks, 1)
            v.wait_ge(g_ps, 1)
            nc.vector.tensor_tensor_reduce(out=junk[:, 0:D], in0=pq[0][0:D, 0:D], in1=ident[0:D, 0:D],
                                           scale=1.0, scalar=0.0, op0=ALU.mult, op1=ALU.add,
                                           accum_out=small[:, 0:1]).then_inc(gdiag, 1)
            for h in range(2):
                nc.vector.tensor_copy(gs[:, h * D:(h + 1) * D], pq[0][0:D, 0:D])
            v.wait_ge(groot, 1)
            v.wait_ge(dv, out_(nc.vector.reciprocal(small[:, 2:3], small[:, 1:2])))
            start_x().then_inc(qr_sb, 1)

            v.wait_ge(p_hi, 1)
            nc.vector.tensor_tensor(phl[:, :, 1, :], pcs[:, :, :], phl[:, :, 0, :].bitcast(F32), ALU.subtract).then_inc(p_lo, 1)

            v.wait_ge(exp_done, 1)
            v.wait_ge(dv, out_(nc.vector.tensor_scalar(cexp[:, :, :], cexp[:, :, :], 1.0, None, ALU.add)))
            v.wait_ge(dv, out_(nc.vector.reciprocal(cexp[:, :, :], cexp[:, :, :])))
            nc.vector.tensor_tensor(silu[0:KC, :, :], cnd[:, :, :], cexp[:, :, :], ALU.mult).then_inc(silu_done, 1)

            def v_out(n):
                r, j0 = n // 2, n % 2 * JH
                v.wait_ge(v_mm, n + 1)
                nc.vector.transpose(vt[:, r, :, j0:j0 + JH].rearrange("p b j -> p j b"),
                                    pe_[n][0:NB, :].rearrange("p (j i) -> p j i", j=JH)).then_inc(vt_sb, 1)

            v.wait_ge(masks, 4)
            with v.Fori(0, NEWTON // 2 - 1) as i:
                for r in range(2):
                    newton_dve(v, qr_mm, qr_sb, i * 6 + 3 * r)
                    x_low(v, i * 2 + r, r)
            v.wait_ge(masks, 7)
            newton_dve(v, qr_mm, qr_sb, 3 * (NEWTON - 2))
            x_low(v, NEWTON - 2, 0)
            newton_dve(v, qr_mm, qr_sb, 3 * (NEWTON - 1), check=True)
            x_low(v, NEWTON - 1, 1)
            v_out(0)
            v.wait_ge(gdiag, 2)
            nc.vector.tensor_reduce(stats[:, 0:1], junk[:, 0:D], AX.X, ALU.max, apply_absolute_value=True)
            k = 3 * NEWTON + 1
            q1_dve(v, qr_mm, k, qr_sb, dv, count[0])
            count[0] += 2

            def mirror():
                v.wait_ge(v1_sb, 4)
                nc.vector.transpose(v2[:, :, :].rearrange("p q j -> p (q j)"), v1[:, :, :].rearrange("p q j -> p (q j)")).then_inc(v2_sb, 1)

            def triangles():
                v.wait_ge(v2_sb, 1)
                for dst, src, mask in ((tri1, v1, upm), (tri2, v2, lom)):
                    out_(nc.vector.tensor_tensor(dst, src, mask[:, :].rearrange("p (a j) -> p a j", a=1).to_broadcast([128, NQ, Q]), ALU.mult))
                tri_count.append(count[0])

            def upper_blocks():
                v.wait_ge(dv, tri_count[0])
                for h in range(2):
                    rows = slice(h * D, h * D + Q)
                    nc.vector.tensor_tensor(zb[rows, :, 1, 0:Q], tri1[rows, :, :], tri2[rows, :, :], ALU.subtract).then_inc(b_sb, 1)

            def lower_blocks():
                v.wait_ge(tri_pool, 2)
                for h in range(2):
                    rows, other = slice(h * D, h * D + Q), slice(h * D + Q, (h + 1) * D)
                    nc.vector.tensor_tensor(zb[other, :, 1, Q:D], tri3[rows, :, :], tri4[rows, :, :], ALU.subtract).then_inc(b_sb, 1)

            tri_count = []
            behind = {1: lambda: v_out(1), 4: lambda: v_out(2), 7: lambda: v_out(3), 8: mirror, 9: triangles, 10: upper_blocks}

            for i in range(SWEEPS):
                sweep_dve(v, qr_mm, k + 1 + i, qr_sb, dv, count[0], ul)
                count[0] += SWEEP_DV
                if NEWTON + i < NG:
                    x_low(v, NEWTON + i, i % 2)
                if i in behind:
                    behind[i]()
            k += SWEEPS + 1
            sweep_dve(v, qr_mm, k, qr_sb, dv, count[0], ul2)
            count[0] += SWEEP_DV
            lower_blocks()
            v.wait_ge(b_sb, 8)
            v.wait_ge(bdb_clear, 1)
            nc.vector.tensor_copy(bdb[0:D, :, 0:D], zb[0:D, :, 1, :]).then_inc(bd0, 1)
            v.wait_ge(vss_mm, 1)
            for h in range(2):
                last = out_(nc.vector.tensor_reduce(vss[:, h * NQ:(h + 1) * NQ], py[h][:, :].rearrange("p (q j) -> p q j", q=NQ),
                                                    AX.X, ALU.add))
            v.wait_ge(dv, last)
            v.wait_ge(dv, out_(nc.vector.tensor_reduce(cnt[:, :], vss[:, :], AX.X, ALU.max)))
            nc.vector.tensor_scalar(more[0:1, 0:1], cnt[0:1, :], NORM_LIMIT ** 2, None, ALU.is_gt).then_inc(more_sb, 1)
            v.wait_ge(dv, out_(nc.vector.tensor_scalar(fac[:, :], cnt[:, :], NORM_LIMIT ** 2, 2.0 ** -EXTRA - 1.0, ALU.is_gt, ALU.mult)))
            v.wait_ge(dv, out_(nc.vector.tensor_scalar(fac[:, :], fac[:, :], 1.0, None, ALU.add)))
            nc.vector.scalar_tensor_tensor(out=nfac2[:, :], in0=fac[:, :], scalar=-1.0, in1=fac[:, :], op0=ALU.mult, op1=ALU.mult).then_inc(fac_sb, 1)
            v.wait_ge(qr_sb, k + 1)
            v.wait_ge(dv, out_(nc.vector.tensor_tensor(junk[:, :], ul[:, :], ul2[:, :], ALU.subtract)))
            v.wait_ge(dv, out_(nc.vector.tensor_scalar(small[:, 4:5], hp[:, :], 2.0, 1.0, ALU.mult, ALU.add)))
            v.wait_ge(dv, out_(nc.vector.tensor_reduce(small[:, 5:6], junk[:, :], AX.X, ALU.max, apply_absolute_value=True)))
            v.wait_ge(dv, out_(nc.vector.tensor_scalar(stats[:, 1:2], small[:, 5:6], SIGN_MARGIN, None, ALU.mult)))
            nc.vector.tensor_reduce(stats[:, 2:3], small[:, 4:5], AX.X, ALU.max, apply_absolute_value=True, negate=True).then_inc(st_sb, 1)
            def diag_from_psum(dst, g):
                qs = slice(g * PG, (g + 1) * PG)
                for h in range(2):
                    last = nc.vector.tensor_scalar(
                        dst[h * D:(h + 1) * D, qs, h * D:(h + 1) * D],
                        pe_[g][h * D:(h + 1) * D, 0:PG * D].rearrange("p (q d) -> p q d", q=PG),
                        nfac2[h * D:(h + 1) * D, 0:1], None, ALU.mult)
                return last

            v.wait_ge(bdz_clear, 2)
            v.wait_ge(fac_sb, 1)
            for g in range(NPG):
                v.wait_ge(ex_act, g + 1)
                diag_from_psum(bdz, g).then_inc(ex_dve, 1)
            for g in range(NPG):
                qs = slice(g * PG, (g + 1) * PG)
                v.wait_ge(ex_act, NPG + g + 1)
                for h in range(2):
                    hs = slice(h * D, (h + 1) * D)
                    nc.vector.tensor_copy(bdz2[hs, qs, hs], zz[hs, qs, 0, :])
                for k, ratio in ((0, C6 / C5), (1, S5 / S4)):
                    last = nc.vector.scalar_tensor_tensor(out=r1[:, qs, k, :], in0=zz[:, qs, k, :], scalar=ratio, in1=zb[:, qs, k, :],
                                                          op0=ALU.mult, op1=ALU.add)
                last.then_inc(ex_dve, 1)
            v.wait_ge(ex_mm, 2 * NPG)
            for k, ratio in ((0, C4 / C3), (1, S3 / S2)):
                last = out_(nc.vector.scalar_tensor_tensor(out=mid[:, :, k, :], in0=zz[:, :, k, :], scalar=ratio, in1=zb[:, :, k, :],
                                                           op0=ALU.mult, op1=ALU.add))
            v.wait_ge(dv, last)
            for g in range(NPG):
                qs = slice(g * PG, (g + 1) * PG)
                pg = pe_[g][:, :].rearrange("p (q k d) -> p q k d", q=PG, k=2)
                v.wait_ge(ex_mm, 2 * NPG + g + 1)
                for k, factor in ((0, C5 / C3), (1, S4 / S2)):
                    last = nc.vector.scalar_tensor_tensor(out=r1[:, qs, k, :], in0=pg[:, :, k, :], scalar=factor,
                                                          in1=mid[:, qs, k, :], op0=ALU.mult, op1=ALU.add)
                last.then_inc(ex_dve, 1)
            v.wait_ge(low_sb, 2)
            for g in range(NPG):
                qs = slice(g * PG, (g + 1) * PG)
                pg = pe_[g][:, :].rearrange("p (q k d) -> p q k d", q=PG, k=2)
                v.wait_ge(ex_mm, 3 * NPG + g + 1)
                for k, factor in ((0, -2 * C3), (1, S2)):
                    last = nc.vector.scalar_tensor_tensor(out=sc[:, qs, k, :], in0=pg[:, :, k, :], scalar=factor,
                                                          in1=sc[:, qs, k, :], op0=ALU.mult, op1=ALU.add)
                last.then_inc(ex_dve, 1)
            def double(lv):
                for g in range(NPG):
                    qs = slice(g * PG, (g + 1) * PG)
                    pg = pe_[g][:, :].rearrange("p (q k d) -> p q k d", q=PG, k=2)
                    v.wait_ge(ex_mm, lv * NPG + (4 * NPG + g + 1))
                    nc.vector.scalar_tensor_tensor(out=sc[:, qs, 1, :], in0=sc[:, qs, 1, :], scalar=2.0, in1=pg[:, :, 0, :],
                                                   op0=ALU.mult, op1=ALU.add).then_inc(ex_dve, 1)

            double(0)
            v.wait_ge(st_mm, 1)
            v.wait_ge(dv, out_(nc.vector.tensor_reduce(st1[0:1, 0:3], pq[1][0:1, 0:3 * D].rearrange("p (k d) -> p k d", k=3), AX.X, ALU.max)))
            v.wait_ge(dv, out_(nc.vector.tensor_tensor(st1[0:1, 3:4], st1[0:1, 1:2], st1[0:1, 2:3], ALU.add)))
            v.wait_ge(dv, out_(nc.vector.tensor_scalar(st1[0:1, 4:5], st1[0:1, 3:4], 0.0, None, ALU.is_le)))
            v.wait_ge(dv, out_(nc.vector.scalar_tensor_tensor(out=st1[0:1, 5:6], in0=st1[0:1, 0:1], scalar=NEWTON_TOL,
                                                              in1=st1[0:1, 4:5], op0=ALU.is_le, op1=ALU.mult)))
            nc.vector.tensor_scalar(redo_qr[0:1, 0:1], st1[0:1, 5:6], -1.0, 1.0, ALU.mult, ALU.add).then_inc(flags, 1)
            v.wait_ge(flags, 1)
            v.wait_ge(more_sb, 1)
            deeper = v.value_load(more[0:1, 0:1], min_val=0, max_val=1)
            redo = v.value_load(redo_qr[0:1, 0:1], min_val=0, max_val=1)
            with v.If(redo):
                general_dve(v)
            for h in range(2):
                last = nc.vector.tensor_copy(xd[:, h, :], xx[:, 0:D])
            last.then_inc(final, 1)
            nc.vector.tensor_scalar(sg[0:D, :], uh[:, :], 0.0, -2.0, ALU.is_ge, ALU.mult).then_inc(final, 1)
            nc.vector.tensor_scalar(sg[D:128, :], uh[:, :], 0.0, -2.0, ALU.is_ge, ALU.mult).then_inc(final, 1)
            v.wait_ge(final, 3)
            nc.vector.tensor_scalar(sg[:, :], sg[:, :], 1.0, None, ALU.add).then_inc(final, 1)
            v.wait_ge(final, 4)
            for h in range(2):
                for k in range(2):
                    nc.vector.tensor_scalar(bdx[h * D:(h + 1) * D, k * D:(k + 1) * D], xx[:, D:2 * D], sg[0:D, 0:1], None,
                                            ALU.mult).then_inc(final, 1)
            with v.Fori(1, LEVELS) as lv:
                double(lv)
            v.wait_ge(uu_mm, 1)
            nc.vector.tensor_scalar(uuh[:, :], pq[1][:, 0:N], sg[:, 0:1], None, ALU.mult).then_inc(uu_sb, 1)
            v.wait_ge(uu_sb, 1)
            nc.vector.scalar_tensor_tensor(out=uul[:, :], in0=pq[1][:, 0:N], scalar=sg[:, 0:1], in1=uuh[:, :].bitcast(F32),
                                           op0=ALU.mult, op1=ALU.subtract).then_inc(uu_sb, 1)

            v.wait_ge(ex_act, (3 + LEVELS) * NPG)
            v.wait_ge(ex_pool, (1 + LEVELS) * NPG)
            v.wait_ge(ex_dve, (4 + LEVELS) * NPG)
            with v.If(deeper):
                with v.Fori(0, EXTRA) as lv:
                    for g in range(NPG):
                        qs = slice(g * PG, (g + 1) * PG)
                        pg = pe_[g][:, :].rearrange("p (q k d) -> p q k d", q=PG, k=2)
                        v.wait_ge(xtra_mm, lv * NPG + (g + 1))
                        nc.vector.scalar_tensor_tensor(out=sc[:, qs, 1, :], in0=sc[:, qs, 1, :], scalar=2.0, in1=pg[:, :, 0, :],
                                                       op0=ALU.mult, op1=ALU.add).then_inc(xtra_sb, 1)
                        nc.vector.tensor_scalar(sc[:, qs, 0, :], pg[:, :, 1, :], 4.0, None, ALU.mult)
                        v.wait_ge(xtra_sb, lv * (2 * NPG) + (2 * g + 1))
                        for h in range(2):
                            hs = slice(h * D, (h + 1) * D)
                            last = nc.vector.tensor_copy(bdb[hs, qs, hs], sc[hs, qs, 1, :])
                        last.then_inc(xtra_sb, 1)
                v.wait_ge(xtra_sb, 2 * NPG * EXTRA)
            for k in range(2):
                qs = slice(k * 8, (k + 1) * 8)
                nc.vector.scalar_tensor_tensor(out=em[:, qs, :], in0=sc[:, qs, 0, :], scalar=-0.5, in1=sc[:, qs, 1, :],
                                               op0=ALU.mult, op1=ALU.add).then_inc(em_sb, 1)
            def f_low(k):
                v.wait_ge(f_hi, k + 1)
                nc.vector.tensor_tensor(fl[:, k * 8:(k + 1) * 8, :, :], f_twice(k), fh[:, k * 8:(k + 1) * 8, :, :].bitcast(F32),
                                        ALU.subtract).then_inc(f_lo, 1)

            def y_low(g):
                v.wait_ge(y_hi, g + 1)
                nc.vector.tensor_tensor(ys[:, 0, 1, :], y[:, g, :], ys[:, 0, 0, :].bitcast(F32), ALU.subtract).then_inc(y_lo_dve, 1)

            y_low(0)
            f_low(0)
            for g in range(NG + 1):
                if g < NG:
                    v.wait_ge(w_hi, g + 1)
                    nc.vector.tensor_tensor(wst[D:128, g % 2, :], py[g % 2][D:128, :], wst[D:128, g % 2, :].bitcast(F32),
                                            ALU.subtract).then_inc(w_lo, 1)
                if g == 0:
                    f_low(1)
                if g >= 1:
                    for c in range(2):
                        v.wait_ge(o_mm, 3 * (g - 1) + c + 1)
                        nc.vector.tensor_tensor(x[:, g - 1, c, :], out_banks[(g - 1) % 2][c][0:KC, :], x[:, g - 1, c, :],
                                                ALU.add).then_inc(o_dve, 1)
                if g == 1:
                    f_low(2)
                    f_low(3)
                if g % 2 == 0 and g + 2 < NG:
                    y_low(g + 2)

        @block.tensor
        def _(pe):
            def keep_clock(n, bank=pe_[3]):
                for _ in range(n):
                    nc.tensor.matmul(bank[:, :], idle[:, 0:128], idle[:, :], start=True, stop=True)

            pe.wait_ge(idle_ones, 1)
            keep_clock(IDLE_START)
            pe.wait_ge(p_in, 16)
            for c in range(NC):
                last = nc.tensor.matmul(pq[0][0:D, 0:D], pcs[:, c, :], pcs[:, c, :], start=(c == 0), stop=(c == NC - 1))
            last.then_inc(g_ps, 1)

            def y_part(g, r, c, k):
                if k == 0 and c == 0 and g >= 2:
                    pe.wait_ge(y_sb, g - 1)
                if k == 0 and c < 2:
                    pe.wait_ge(x_lo_pool, 2 * g + c + 1)
                if k == 0 and c == 2:
                    pe.wait_ge(x_lo_dve, g + 1)
                ins = nc.tensor.matmul(py[r][:, :], phl[:, c, :, :].rearrange("p k d -> p (k d)"), xs[:, r, c, k, :],
                                       start=(c == 0 and k == 0), stop=(c == NC - 1 and k == 1))
                if k == 1:
                    ins.then_inc(xs_used, 1)

            def y_chunk(g, r, c):
                for k in range(2):
                    y_part(g, r, c, k)

            def block_fill(g, r):
                it = iter(range(NC))

                def fill():
                    y_chunk(g, r, next(it))
                    keep_clock(IDLE_N)
                return fill

            def v_product(m):
                n, c = m // NC, m % NC
                if c == 0:
                    pe.wait_ge(w_in[n], 16)
                kc = KC + 1 if c == 0 else KC
                ins = nc.tensor.matmul(pe_[n][0:NB, :], silu[0:kc, c, :], wq[0:kc, c, n, :], start=(c == 0), stop=(c == NC - 1))
                if c == NC - 1:
                    ins.then_inc(v_mm, 1)

            pe.wait_ge(masks, 4)
            keep_clock(IDLE_G)
            newton_pe(pe, qr_mm, qr_sb, 1, lambda: keep_clock(IDLE_N0))
            pe.wait_ge(p_lo, 1)
            pe.wait_ge(silu_done, 1)
            pe.wait_ge(b_in, 16)
            for j in range(2):
                newton_pe(pe, qr_mm, qr_sb, 4 + 3 * j, block_fill(j, j))
                v_product(j)
            for j in range(3):
                newton_pe(pe, qr_mm, qr_sb, 10 + 3 * j, block_fill(2 + j, j % 2))
                v_product(j + 2)
            pe.wait_ge(pt_in, 16)
            k = 3 * NEWTON + 1
            pe.wait_ge(qr_sb, k)
            q1_pe(qr_mm)
            for j in range(SWEEPS):
                sweep_pe(pe, qr_mm, qr_sb, k + 1 + j)
                if j + NEWTON - 1 < NG:
                    for c in range(NC):
                        y_chunk(j + NEWTON - 1, (j + NEWTON - 1) % 2, c)
                if j + NEWTON - 1 < NC * NV:
                    v_product(j + NEWTON - 1)
                else:
                    pe.wait_ge(vt_sb, 1)
                    keep_clock(IDLE_S2 if j + NEWTON - 1 < NG else IDLE_S3, pe_[0])
            k += SWEEPS + 1
            sweep_pe(pe, qr_mm, qr_sb, k)
            keep_clock(IDLE_S3, pe_[0])
            pe.wait_ge(vsq_done, 1)
            pe.wait_ge(y_sb, NG)
            for h in range(2):
                last = nc.tensor.matmul(py[h][:, :], onesm[h * D:(h + 1) * D, :], vsq[h * D:(h + 1) * D, :], start=True, stop=True)
            last.then_inc(vss_mm, 1)
            def products(g, left, right, done, idle_after=0):
                if idle_after:
                    keep_clock(idle_after)
                for q in range(PG):
                    p = g * PG + q
                    last = nc.tensor.matmul(pe_[g][:, q * 2 * D:(q + 1) * 2 * D], left[:, p, :],
                                            right[:, p, :, :].rearrange("p k d -> p (k d)"), start=True, stop=True)
                last.then_inc(done, 1)

            keep_clock(IDLE_B, pe_[0])
            pe.wait_ge(bd0, 2)
            for g in range(NPG):
                for q in range(PG):
                    last = nc.tensor.matmul(pe_[g][:, q * D:(q + 1) * D], bdb[:, g * PG + q, :], zb[:, g * PG + q, 1, :],
                                            start=True, stop=True)
                last.then_inc(ex_mm, 1)
            pe.wait_ge(st_sb, 1)
            for j in range(3):
                last = nc.tensor.matmul(pq[1][0:1, j * D:(j + 1) * D], stats[:, j:j + 1], ident[0:D, 0:D], start=True, stop=True)
            last.then_inc(st_mm, 1)
            keep_clock(IDLE_1, pq[0])
            for g in range(NPG):
                pe.wait_ge(ex_dve, g + 1)
                pe.wait_ge(b_scaled, g + 1)
                products(g, bdz, zb, ex_mm)
            keep_clock(IDLE_2, pq[0])
            for g in range(NPG):
                pe.wait_ge(ex_dve, NPG + g + 1)
                products(g, bdz2, r1, ex_mm)
            keep_clock(IDLE_3, pq[0])
            for g in range(NPG):
                pe.wait_ge(ex_dve, 2 * NPG + g + 1)
                products(g, bdz2, r1, ex_mm)
            keep_clock(IDLE_4, pq[0])

            def double(lv):
                for g in range(NPG):
                    pe.wait_ge(ex_act, lv * NPG + (2 * NPG + g + 1))
                    pe.wait_ge(ex_pool, lv * NPG + (g + 1))
                    products(g, bdb, sc, ex_mm)

            double(0)
            double(1)
            pe.wait_ge(more_sb, 1)
            deeper = pe.value_load(more[0:1, 0:1], min_val=0, max_val=1)
            pe.wait_ge(flags, 1)
            redo = pe.value_load(redo_qr[0:1, 0:1], min_val=0, max_val=1)
            with pe.If(redo):
                general_pe(pe)
            for lv in range(2, LEVELS):
                double(lv)
            pe.wait_ge(final, 1)
            nc.tensor.matmul(pq[1][:, 0:N], xd[:, :, :].rearrange("p k d -> p (k d)"), pts[:, :],
                             start=True, stop=True).then_inc(uu_mm, 1)

            pe.wait_ge(ex_pool, NPG * (1 + LEVELS))
            pe.wait_ge(ex_act, (3 + LEVELS) * NPG)
            with pe.If(deeper):
                for g in range(NPG):
                    products(g, bdb, sc, xtra_mm)
                with pe.Fori(1, EXTRA) as lv:
                    for g in range(NPG):
                        pe.wait_ge(xtra_sb, lv * (2 * NPG) + (2 * g + 2 - 2 * NPG))
                        products(g, bdb, sc, xtra_mm)
            def f_products(k):
                h, q0 = k // 2, k % 2 * 8
                nc.tensor.matmul(pe_[k][:, :], bdx[h * D:(h + 1) * D, :],
                                 em[h * D:(h + 1) * D, q0:q0 + 8, :].rearrange("p q d -> p (q d)"), start=True, stop=True).then_inc(f_mm, 1)

            pe.wait_ge(final, 8)
            keep_clock(IDLE_E, pq[0])
            for k in range(4):
                pe.wait_ge(em_sb, k % 2 + 1)
                f_products(k)
            pe.wait_ge(uu_sb, 2)
            keep_clock(IDLE_F, pq[0])

            for g in range(NG + 1):
                if g < NG:
                    pe.wait_ge(y_lo_dve, g // 2 + 1)
                    if g % 2:
                        pe.wait_ge(y_lo_pool, g // 2 + 1)
                    if g >= 2:
                        pe.wait_ge(w_lo, g - 1)
                    if g % 4 == 0:
                        pe.wait_ge(f_lo, g // 4 + 1)
                    for r in range(GB):
                        b = g * GB + r
                        for k in range(2):
                            for f in (fh, fl):
                                last = nc.tensor.matmul(py[g % 2][:, r * T:(r + 1) * T],
                                                        f[:, b, :, :].rearrange("p k d -> p (k d)"),
                                                        ys[:, g % 2, k, r * T:(r + 1) * T],
                                                        start=(k == 0 and f is fh), stop=(k == 1 and f is fl))
                    last.then_inc(w_mm, 1)
                if g >= 1:
                    k = g - 1
                    pe.wait_ge(w_lo, k + 1)
                    for c in range(NC):
                        bank = out_banks[k % 2][c]
                        if k < 2 and bank in pe_:
                            pe.wait_ge(f_lo, pe_.index(bank) + 1)
                        if c < 2 and k >= 2:
                            pe.wait_ge(o_dve, 2 * (k - 2) + c + 1)
                        if c == 2 and k >= 2:
                            pe.wait_ge(o_act, k - 1)
                        for j, uu in enumerate((uuh, uul)):
                            last = nc.tensor.matmul(bank[0:KC, :], uu[:, c * KC:(c + 1) * KC], wst[:, k % 2, :],
                                                    start=(j == 0), stop=(j == 1))
                        last.then_inc(o_mm, 1)


def kernel(x, cond_1152, L0_cond_P, L0_cond_W, L0_cond_b):
    import numpy as np
    import concourse.bacc as bacc
    from concourse.bass_utils import run_bass_kernel_spmd

    xb = np.ascontiguousarray(np.asarray(x).reshape(NG, BT, NC, KC).transpose(0, 3, 2, 1))
    cond = np.ascontiguousarray(np.asarray(cond_1152).reshape(NB, NC, KC).transpose(2, 1, 0))
    P = np.asarray(L0_cond_P)
    pc = np.ascontiguousarray(P.reshape(NC, KC, D).transpose(1, 0, 2))
    pt = np.ascontiguousarray(P.T)
    iu, ju = np.triu_indices(D, k=1)
    where = np.zeros((D, D), np.int64)
    where[iu, ju] = where[ju, iu] = np.arange(len(iu))
    low = np.tri(Q, dtype=bool)
    folded = np.where(low, where[Q:, Q:], where[:Q, :Q])
    where = np.stack([folded, where[:Q, Q:]]).transpose(0, 2, 1).reshape(NV, BANK)
    W = np.asarray(L0_cond_W)
    wd = np.ascontiguousarray(W[where].reshape(NV, BANK, NC, KC).transpose(3, 2, 0, 1))
    bd = np.ascontiguousarray(np.asarray(L0_cond_b)[where][None])

    nc = bacc.Bacc("TRN2", target_bir_lowering=False, num_devices=1)
    arrays = {"xb": xb, "cond": cond, "pc": pc, "pt": pt, "wd": wd, "bd": bd}
    args = [nc.dram_tensor(k, a.shape, mybir.dt.from_np(a.dtype), kind="ExternalInput").ap() for k, a in arrays.items()]
    out = nc.dram_tensor("out", xb.shape, F32, kind="ExternalOutput").ap()
    rotation_kernel(nc, *args, out)
    r = run_bass_kernel_spmd(nc, [arrays], core_ids=[0])
    got = r.results[0]["out"]
    return np.ascontiguousarray(got.transpose(0, 3, 2, 1)).reshape(NB, T, N)
```
